# Optimizing a Trainium2 kernel written in Bass

```python
import numpy as np
import jax
import jax.numpy as jnp

def _softmax(x, axis=-1):
    return jax.nn.softmax(x, axis=axis)

def _gelu(x):
    return jax.nn.gelu(x, approximate=True)

def _silu(x):
    return jax.nn.silu(x)

def _sigmoid(x):
    return jax.nn.sigmoid(x)

def _layernorm(x, axis=-1, eps=1e-05):
    m = jnp.mean(x, axis=axis, keepdims=True)
    v = jnp.var(x, axis=axis, keepdims=True)
    return (x - m) / jnp.sqrt(v + eps)

def _scatter_add(tgt, idx, src, axis=0):
    return tgt.at[idx].add(src)

def _segment_sum(src, seg, n):
    return jax.ops.segment_sum(src, seg, n)
kernel_name = 'mk_vit_tower_cls_d1_tok_img768_r4_e1ae6b'

def setup_inputs(seed: int=0):
    np.random.seed(seed)
    _w = jnp.asarray

    def _rec_inputs():
        import jax
        import jax.numpy as jnp
        _rk = jax.random.key(seed)
        x = 7.57192e-06 + 1.00007 * jax.random.normal(jax.random.fold_in(_rk, 1), (128, 3, 224, 224), jnp.float32)
        cls_tok = 0.02 * jax.random.normal(jax.random.fold_in(_rk, 5), (1, 1, 192), jnp.float32)
        return (x, cls_tok)
    x, cls_tok = _rec_inputs()

    def _L0_tok_setup():
        import jax, jax.numpy as jnp
        import numpy as np
        IMG = 224
        P = 16
        C = 3
        D = 192
        GH = IMG // P
        NP_ = GH * GH
        PATCH_DIM = P * P * C
        EPS = 1e-05

        def _patchify(x):
            B = x.shape[0]
            x = x.reshape(B, C, GH, P, GH, P)
            x = x.transpose(0, 2, 4, 1, 3, 5)
            return x.reshape(B, NP_, PATCH_DIM)
        key = jax.random.key(seed)
        ks = jax.random.split(key, 5)
        x = jax.random.normal(ks[0], (64, C, IMG, IMG), dtype=jnp.float32)
        W1 = jax.random.normal(ks[1], (PATCH_DIM, D), dtype=jnp.float32) / np.sqrt(PATCH_DIM)
        b1 = jnp.zeros((D,), dtype=jnp.float32)
        ln_w = jnp.ones((D,), dtype=jnp.float32)
        ln_b = jnp.zeros((D,), dtype=jnp.float32)
        W2 = jax.random.normal(ks[2], (D, D), dtype=jnp.float32) / np.sqrt(D)
        b2 = jnp.zeros((D,), dtype=jnp.float32)
        return {'x': x, 'W1': W1, 'b1': b1, 'ln_w': ln_w, 'ln_b': ln_b, 'W2': W2, 'b2': b2}
    _L0_tok_all = _L0_tok_setup()
    _L0_tok_in = {k: v for k, v in _L0_tok_all.items() if k in ('W1', 'b1', 'ln_w', 'ln_b', 'W2', 'b2')}
    del _L0_tok_all

    def _L0_attn_setup():
        import jax, jax.numpy as jnp
        import numpy as np
        NUM_HEADS = 12
        NEG = -1000000000.0
        key = jax.random.key(seed)
        ks = jax.random.split(key, 5)
        B, S, D = (4, 512, 192)
        scale = 0.02
        return {'x': jax.random.normal(ks[0], (B, S, D), dtype=jnp.float32), 'wq': jax.random.normal(ks[1], (D, D), dtype=jnp.float32) * scale, 'wk': jax.random.normal(ks[2], (D, D), dtype=jnp.float32) * scale, 'wv': jax.random.normal(ks[3], (D, D), dtype=jnp.float32) * scale, 'wo': jax.random.normal(ks[4], (D, D), dtype=jnp.float32) * scale}
    _L0_attn_all = _L0_attn_setup()
    _L0_attn_in = {k: v for k, v in _L0_attn_all.items() if k in ('wq', 'wk', 'wv', 'wo')}
    del _L0_attn_all

    def _L0_ffn_setup():
        import jax, jax.numpy as jnp
        import numpy as np
        DIM = 192
        NUM_HEADS = 12
        HEAD_DIM = DIM // NUM_HEADS
        SCALE = HEAD_DIM ** (-0.5)
        NUM_EXPERTS = 8
        RANK = 16
        ALPHA = 32
        TOPK = 2
        SCALING = ALPHA / RANK
        B, S = (8, 256)
        key = jax.random.key(seed)
        ks = jax.random.split(key, 12)
        d, e, r = (DIM, NUM_EXPERTS, RANK)
        inp = {'x': jax.random.normal(ks[0], (B, S, d), jnp.float32), 'Wg': jax.random.normal(ks[1], (e, d), jnp.float32) * 0.02, 'bg': jax.random.normal(ks[2], (e,), jnp.float32) * 0.02, 'Wqkv': jax.random.normal(ks[3], (3 * d, d), jnp.float32) * 0.02, 'bqkv': jax.random.normal(ks[4], (3 * d,), jnp.float32) * 0.02, 'Wproj': jax.random.normal(ks[5], (d, d), jnp.float32) * 0.02, 'bproj': jax.random.normal(ks[6], (d,), jnp.float32) * 0.02, 'A': jax.random.normal(ks[7], (e, r, d), jnp.float32) * 0.05, 'ba': jax.random.normal(ks[8], (e, r), jnp.float32) * 0.02, 'Bm': jax.random.normal(ks[9], (e, 3 * d, r), jnp.float32) * 0.05, 'bb': jax.random.normal(ks[10], (e, 3 * d), jnp.float32) * 0.02}
        return inp
    _L0_ffn_all = _L0_ffn_setup()
    _L0_ffn_in = {k: v for k, v in _L0_ffn_all.items() if k in ('Wg', 'bg', 'Wqkv', 'bqkv', 'Wproj', 'bproj', 'A', 'ba', 'Bm', 'bb')}
    del _L0_ffn_all
    return {'x': x, 'cls_tok': cls_tok, 'L0_tok_W1': _L0_tok_in['W1'], 'L0_tok_b1': _L0_tok_in['b1'], 'L0_tok_ln_w': _L0_tok_in['ln_w'], 'L0_tok_ln_b': _L0_tok_in['ln_b'], 'L0_tok_W2': _L0_tok_in['W2'], 'L0_tok_b2': _L0_tok_in['b2'], 'L0_attn_wq': _L0_attn_in['wq'], 'L0_attn_wk': _L0_attn_in['wk'], 'L0_attn_wv': _L0_attn_in['wv'], 'L0_attn_wo': _L0_attn_in['wo'], 'L0_ffn_Wg': _L0_ffn_in['Wg'], 'L0_ffn_bg': _L0_ffn_in['bg'], 'L0_ffn_Wqkv': _L0_ffn_in['Wqkv'], 'L0_ffn_bqkv': _L0_ffn_in['bqkv'], 'L0_ffn_Wproj': _L0_ffn_in['Wproj'], 'L0_ffn_bproj': _L0_ffn_in['bproj'], 'L0_ffn_A': _L0_ffn_in['A'], 'L0_ffn_ba': _L0_ffn_in['ba'], 'L0_ffn_Bm': _L0_ffn_in['Bm'], 'L0_ffn_bb': _L0_ffn_in['bb']}

def reference(x, cls_tok, L0_tok_W1, L0_tok_b1, L0_tok_ln_w, L0_tok_ln_b, L0_tok_W2, L0_tok_b2, L0_attn_wq, L0_attn_wk, L0_attn_wv, L0_attn_wo, L0_ffn_Wg, L0_ffn_bg, L0_ffn_Wqkv, L0_ffn_bqkv, L0_ffn_Wproj, L0_ffn_bproj, L0_ffn_A, L0_ffn_ba, L0_ffn_Bm, L0_ffn_bb):
    import jax
    import jax.numpy as jnp

    def _L0_tok_ref(x, W1, b1, ln_w, ln_b, W2, b2):
        import jax, jax.numpy as jnp
        import numpy as np
        IMG = 224
        P = 16
        C = 3
        D = 192
        GH = IMG // P
        NP_ = GH * GH
        PATCH_DIM = P * P * C
        EPS = 1e-05

        def _patchify(x):
            B = x.shape[0]
            x = x.reshape(B, C, GH, P, GH, P)
            x = x.transpose(0, 2, 4, 1, 3, 5)
            return x.reshape(B, NP_, PATCH_DIM)
        patches = _patchify(x)
        h = jnp.einsum('bnd,de->bne', patches, W1) + b1
        mu = jnp.mean(h, axis=-1, keepdims=True)
        var = jnp.mean(jnp.square(h - mu), axis=-1, keepdims=True)
        h = (h - mu) * jax.lax.rsqrt(var + EPS) * ln_w + ln_b
        h = jax.nn.gelu(h, approximate=False)
        return jnp.einsum('bnd,de->bne', h, W2) + b2

    def _L0_attn_ref(x, wq, wk, wv, wo):
        import jax, jax.numpy as jnp
        import numpy as np
        NUM_HEADS = 12
        NEG = -1000000000.0
        B, S, D = x.shape
        H = NUM_HEADS
        dh = D // H

        def proj(w):
            return (x @ w.T).reshape(B, S, H, dh).transpose(0, 2, 1, 3)
        q, k, v = (proj(wq), proj(wk), proj(wv))
        score = jnp.einsum('bhqd,bhkd->bhqk', q, k) / jnp.float32(np.sqrt(dh))
        causal = jnp.triu(jnp.ones((S, S), dtype=bool), k=1)
        score = score + jnp.where(causal, jnp.float32(NEG), jnp.float32(0.0))
        attn = jax.nn.softmax(score, axis=-1)
        out = jnp.einsum('bhqk,bhkd->bhqd', attn, v)
        out = out.transpose(0, 2, 1, 3).reshape(B, S, D)
        return out @ wo.T

    def _L0_ffn_ref(x, Wg, bg, Wqkv, bqkv, Wproj, bproj, A, ba, Bm, bb):
        import jax, jax.numpy as jnp
        import numpy as np
        DIM = 192
        NUM_HEADS = 12
        HEAD_DIM = DIM // NUM_HEADS
        SCALE = HEAD_DIM ** (-0.5)
        NUM_EXPERTS = 8
        RANK = 16
        ALPHA = 32
        TOPK = 2
        SCALING = ALPHA / RANK
        B, S = (8, 256)
        b, s, d = x.shape
        t = b * s
        xf = x.reshape(t, d)
        probs = jax.nn.softmax(xf @ Wg.T + bg, axis=-1)
        top_w, top_idx = jax.lax.top_k(probs, TOPK)
        combine = jnp.zeros((t, NUM_EXPERTS), x.dtype).at[jnp.arange(t)[:, None], top_idx].add(top_w)
        h = jnp.einsum('td,erd->ter', xf, A) + ba
        hw = h * combine[:, :, None]
        delta = jnp.einsum('ter,eor->to', hw, Bm) + combine @ bb
        delta = delta * SCALING
        qkv = xf @ Wqkv.T + bqkv + delta
        qkv = qkv.reshape(b, s, 3, NUM_HEADS, HEAD_DIM)
        qkv = jnp.transpose(qkv, (2, 0, 3, 1, 4))
        q, k, v = (qkv[0], qkv[1], qkv[2])
        attn = jax.nn.softmax(jnp.einsum('bhsd,bhtd->bhst', q, k) * SCALE, axis=-1)
        out = jnp.einsum('bhst,bhtd->bhsd', attn, v)
        out = jnp.transpose(out, (0, 2, 1, 3)).reshape(b, s, d)
        return out @ Wproj.T + bproj
    h = _L0_tok_ref(x, L0_tok_W1, L0_tok_b1, L0_tok_ln_w, L0_tok_ln_b, L0_tok_W2, L0_tok_b2)
    h = jnp.concatenate([jnp.broadcast_to(cls_tok, (h.shape[0], 1, h.shape[2])), h], axis=1)
    h = h + _L0_attn_ref(_layernorm(h, axis=-1), L0_attn_wq, L0_attn_wk, L0_attn_wv, L0_attn_wo)
    h = h + _L0_ffn_ref(_layernorm(h, axis=-1), L0_ffn_Wg, L0_ffn_bg, L0_ffn_Wqkv, L0_ffn_bqkv, L0_ffn_Wproj, L0_ffn_bproj, L0_ffn_A, L0_ffn_ba, L0_ffn_Bm, L0_ffn_bb)
    return h

_drawn_inputs = setup_inputs


def setup_inputs(seed=0):
    import zlib

    import numpy as np

    out = dict(_drawn_inputs(seed))
    spreads = {'L0_tok_b1': (0.0, 0.1),
     'L0_tok_ln_w': (1.0, 0.2),
     'L0_tok_ln_b': (0.0, 0.1),
     'L0_tok_b2': (0.0, 0.1)}
    factors = {'cls_tok': 5.296,
     'L0_attn_wq': 8.0,
     'L0_attn_wk': 8.0,
     'L0_ffn_Wg': 8.0,
     'L0_ffn_bg': 8.0,
     'L0_ffn_bqkv': 8.0,
     'L0_ffn_A': 5.747,
     'L0_ffn_ba': 8.0,
     'L0_ffn_Bm': 6.953,
     'L0_ffn_bb': 8.0,
     'L0_ffn_bproj': 7.954}
    for name, (base, spread) in spreads.items():
        noise = np.random.default_rng([zlib.crc32(name.encode()), seed]).standard_normal(out[name].shape)
        drawn = base * np.exp(spread * noise) if base else spread * noise
        out[name] = jnp.asarray(drawn.astype(out[name].dtype))
    for name, factor in factors.items():
        out[name] = (out[name] * factor).astype(out[name].dtype)
    return out
```

```python
from contextlib import ExitStack

import concourse.bass as bass
from concourse import mybir

F32 = mybir.dt.float32
BF16 = mybir.dt.bfloat16
ALU = mybir.AluOpType
ACT = mybir.ActivationFunctionType
AX_X = mybir.AxisListType.X

IMAGES, CHANNELS, IMG = 128, 3, 224
PATCH = 16
GRID = IMG // PATCH
D = 192
HEADS, HD = 12, 16
TOK = GRID * GRID + 1
HALF = GRID * GRID // 2
ROWS = [HALF + 1, HALF]
PAIRS = IMAGES // 2
PT = 2 * TOK
FC = D // 2
QH = PATCH // 2
XR = CHANNELS * PATCH
EXPERTS, RANK = 8, 16
ER = EXPERTS * RANK
GH = 4
GROUPS = HEADS // GH
PARTS = 3
SR = 6 * HD
EPS = 1e-5
SCALE = float(HD) ** -0.5
LORA_SCALE = 2.0
BIG = 4.0

Q_RUNS = [(0, 0, 1), (1, 0, 1), (2, 0, 1), (3, 1, 1), (4, 1, 2)]
K_RUNS = [(0, 0, 3), (3, 0, 2), (5, 0, 1)]


class Count:

    def __init__(self, ctx, nc, name, per):
        self.sem = ctx.enter_context(nc.semaphore(name))
        self.per = per

    def at(self, pair, k):
        return pair * self.per + k


def later(pair):
    return not (isinstance(pair, int) and pair == 0)


def tile_cols(t):
    b, a = divmod(t, 2)
    c = b * TOK + a * (HALF + 1)
    return slice(c, c + ROWS[a])


def vit_tower(nc, x, w1, w2, lnp, wqkv1, wo1, wgl, wqkv2, wlora, wo2, ident, identb, masks, sel, marks, rank8, out):
    with ExitStack() as ctx:
        def sb(name, shape, dt=F32):
            return ctx.enter_context(nc.sbuf_tensor(name, shape, dt))

        def cnt(name, per):
            return Count(ctx, nc, name, per)

        def cnt2(name, per):
            return [Count(ctx, nc, f"{name}{s}", per) for s in range(2)]

        ps = ctx.enter_context(nc.psum_tensor("ps", [128, 8, 512], F32))
        dparts = [nc.dram_tensor(f"parts_dram{s}", (2, 2, PARTS, FC, PT), BF16, kind="Internal").ap() for s in range(2)]
        dmax = [nc.dram_tensor(f"max_dram{s}", (2, PARTS * HEADS, TOK), BF16, kind="Internal").ap() for s in range(2)]

        w1_s = sb("w1_s", [XR * 2 + 1, QH, D])
        w2_s = sb("w2_s", [FC + 2, 2, D])
        lnp_s = sb("lnp_s", [FC, 2, 2])
        wqkv_s = [sb("wqkv1_s", [FC, 2, 3 * D]), sb("wqkv2_s", [FC + 1 + EXPERTS, 2, 3 * D])]
        wlora_s = sb("wlora_s", [ER, 3 * D])
        wgl_s = sb("wgl_s", [FC + 1, 2, ER + EXPERTS])
        wo_s = [sb("wo1_s", [128, GROUPS, D]), sb("wo2_s", [128, GROUPS, D])]
        id_s = sb("id_s", [128, 128])
        idb_s = sb("idb_s", [128, 128], BF16)
        mask_s = sb("mask_s", [HALF + 1, 4, HALF + 1], BF16)
        sel_s = sb("sel_s", [128, 128])
        rank_s = sb("rank_s", [HALF + 1, EXPERTS])
        xb = sb("xb", [XR * 2 + 1, 2, GRID, IMG])
        h0n = sb("h0n", [HALF, 4, D])
        gT = sb("gT", [FC + 2, 2, PT])
        h1 = sb("h1", [HALF + 1, 4, D])
        n1 = sb("n1", [HALF + 1, 4, D])
        nT1 = sb("nT1", [FC, 2, PT])
        h2 = sb("h2", [HALF + 1, 4, D])
        n2 = sb("n2", [HALF + 1, 4, D])
        nT2 = sb("nT2", [FC + 1 + EXPERTS, 2, PT])
        hw = sb("hw", [HALF + 1, 4, ER])
        hwT = sb("hwT", [ER, PT])
        outb = sb("outb", [HALF + 1, 4, D])
        st = [sb(f"st{k}", [HALF + 1, 4, 6]) for k in range(3)]
        mv = [sb(f"mv{k}", [HALF + 1, 4, 2]) for k in range(3)]
        ve = [sb(f"ve{k}", [HALF + 1, 4, 1]) for k in range(3)]
        half_s = sb("half_s", [HALF + 1, 2, 1])
        rstd = [sb(f"rstd{k}", [HALF + 1, 4, 1]) for k in range(3)]
        parts = [sb(f"parts{s}", [FC, 4, PARTS, PT], BF16) for s in range(2)]
        rest = sb("rest", [FC, 4, PT])
        Qs = [sb(f"Qs{s}", [SR + PARTS, HEADS, PT], BF16) for s in range(2)]
        Ks = [sb(f"Ks{s}", [SR + PARTS, HEADS, PT], BF16) for s in range(2)]
        V = [sb(f"V{s}", [HALF + 1, 4, HEADS, 32]) for s in range(2)]
        mx = sb("mx", [HALF + 1, 2, 2, HEADS])
        mxr = sb("mxr", [HALF + 1, 2, HEADS])
        mxp = sb("mxp", [HALF + 1, 2, 2, PARTS, HEADS], BF16)
        mT = sb("mT", [PARTS * HEADS, 2, TOK], BF16)
        P = sb("P", [HALF + 1, 4, GH * TOK])
        O = sb("O", [128, GROUPS, PT])
        inv = sb("inv", [128, PT])
        lg = sb("lg", [HALF + 1, 4, EXPERTS])
        pe_ = sb("probs", [HALF + 1, 4, EXPERTS])
        pr = sb("pr", [HALF + 1, 4, EXPERTS])
        ge = sb("ge", [HALF + 1, 4, EXPERTS])
        gc = sb("gc", [HALF + 1, 4, EXPERTS])
        s1 = sb("s1", [HALF + 1, 4, EXPERTS])
        s2 = sb("s2", [HALF + 1, 4, EXPERTS])
        gm = sb("gm", [HALF + 1, 4, 1])
        comb = sb("comb", [HALF + 1, 4, 1 + EXPERTS])

        weights_in = cnt("weights_in", 0)
        init_done = cnt("init_done", 0)
        wait_held = cnt("wait_held", 0)
        x_in = cnt("x_in", 12 * 16)
        patch_mm = cnt("patch_mm", 4)
        h0_normed = cnt("h0_normed", 4)
        h0T_mm = cnt("h0T_mm", 2)
        gelu_done = cnt("gelu_done", 4)
        w2_mm = cnt("w2_mm", 4)
        h1_copied = cnt("h1_copied", 4)
        n1_normed = cnt("n1_normed", 4)
        n1T_mm = cnt("n1T_mm", 4)
        n1T_copied = cnt("n1T_copied", 4)
        qk_mm = cnt2("qk_mm", 4)
        hi_done = cnt2("hi_done", 4)
        rest_done = cnt2("rest_done", 4)
        lo_done = cnt2("lo_done", 4)
        mid_done = cnt2("mid_done", 4)
        parts_out = cnt2("parts_out", 4 * 16)
        stacks_in = cnt2("stacks_in", 8 * 16)
        v_mm = cnt2("v_mm", 4)
        v_copied = cnt2("v_copied", 4)
        p1_mm = cnt2("p1_mm", 12)
        max_done = cnt2("max_done", 12)
        max_parts = cnt2("max_parts", 2)
        mT_mm = cnt2("mT_mm", 2)
        mT_copied = cnt2("mT_copied", 2)
        mT_out = cnt2("mT_out", 2 * 16)
        mT_in = [[cnt(f"mT_in{s}{b}", 16) for b in range(2)] for s in range(2)]
        p2_mm = cnt2("p2_mm", 12)
        exp_done = cnt2("exp_done", 12)
        av_mm = cnt2("av_mm", 6)
        av_copied = cnt2("av_copied", 6)
        sum_mm = cnt2("sum_mm", 3)
        divided = cnt2("divided", 3)
        wo_mm = cnt2("wo_mm", 4)
        added = cnt2("added", 4)
        n2_normed = cnt("n2_normed", 4)
        n2T_mm = cnt("n2T_mm", 4)
        n2T_copied = cnt("n2T_copied", 4)
        gate_mm = cnt("gate_mm", 4)
        logits_done = cnt("logits_done", 1)
        gate_exp = cnt("gate_exp", 1)
        comb_done = cnt("comb_done", 1)
        hw_done = cnt("hw_done", 4)
        hwT_mm = cnt("hwT_mm", 4)
        hwT_copied = cnt("hwT_copied", 4)
        out_stored = cnt("out_stored", 6 * 16)
        dve_stats = [cnt(f"dve_stats{k}", 8) for k in range(3)]
        dve_here = cnt("dve_here", 2 * 2 * 3 + 2 * GROUPS + 18)
        var_done = [cnt(f"var_done{k}", 4) for k in range(3)]
        rstd_done = [cnt(f"rstd_done{k}", 2) for k in range(3)]

        LOADS = [(w1_s[:, :, :], w1), (w2_s[:, :, :], w2), (lnp_s[:, :, :], lnp), (wqkv_s[0][:, :, :], wqkv1),
                 (wo_s[0][:, :, :], wo1), (wgl_s[:, :, :], wgl), (wqkv_s[1][:, :, :], wqkv2), (wlora_s[:, :], wlora),
                 (wo_s[1][:, :, :], wo2), (id_s[:, :], ident), (idb_s[:, :], identb), (mask_s[:, :, :], masks),
                 (sel_s[:, :], sel), (rank_s[:, :], rank8)]
        N_INIT = 16

        def score_slot(z, n, lo, cols):
            return ps[0:n, 2 * z:2 * z + 2, 0:2 * TOK].rearrange("p k (h c) -> p k h c", h=2)[:, :, :, lo:lo + cols]

        block = ctx.enter_context(nc.Block())

        def hold_wait(eng):
            eng.sem_inc(wait_held.sem, 1)

        @block.sync
        def _(sp):
            def load_x(n):
                img = x.rearrange("b c (g p) w -> b c p g w", p=PATCH)
                for b in range(2):
                    for c in range(CHANNELS):
                        for s in range(2):
                            r = XR * s + PATCH * c
                            src = img[bass.ds(2 * n + b, 1), c].rearrange("o p g w -> (o p) g w")
                            sp.dma_start(xb[r:r + PATCH, b, :, 0:IMG - QH * s],
                                         src[:, :, QH * s:IMG]).then_inc(x_in.sem, 16)

            def stack_parts(s, n):
                if later(n):
                    sp.wait_ge(stacks_in[s].sem, stacks_in[s].at(n - 1, stacks_in[s].per))
                hold_wait(sp)
                for m in range(4):
                    sp.wait_ge(lo_done[s].sem, lo_done[s].at(n, m + 1))
                    sp.dma_start(dparts[s][m // 2, m % 2].rearrange("r p c -> p r c"),
                                 parts[s][:, m, :, :]).then_inc(parts_out[s].sem, 16)
                sp.wait_ge(parts_out[s].sem, parts_out[s].at(n, 4 * 16))
                if later(n):
                    sp.wait_ge(p2_mm[s].sem, p2_mm[s].at(n - 1, 12))
                for qk, (stack, runs) in enumerate(((Qs[s], Q_RUNS), (Ks[s], K_RUNS))):
                    for slot, part, k in runs:
                        src = dparts[s][qk].rearrange("m r (j h) c -> (r j) m h c", h=6)
                        sp.dma_start(stack[HD * slot:HD * (slot + k), :, :].rearrange("p (m h) c -> p m (h c)", m=2),
                                     src[HD * part:HD * (part + k)].rearrange("p m h c -> p m (h c)")).then_inc(stacks_in[s].sem, 16)

            def max_rows(s, n, b):
                sp.wait_ge(mT_copied[s].sem, mT_copied[s].at(n, b + 1))
                sp.dma_start(dmax[s][b], mT[:, b, :]).then_inc(mT_out[s].sem, 16)
                sp.wait_ge(mT_out[s].sem, mT_out[s].at(n, 16 * (b + 1)))
                sp.dma_start(Qs[s][SR:SR + PARTS, :, b * TOK:(b + 1) * TOK],
                             dmax[s][b].rearrange("(r h) c -> r h c", r=PARTS)).then_inc(mT_in[s][b].sem, 16)

            def store(n):
                images = [out[bass.ds(sp.snap(2 * n + b), 1)].rearrange("o t d -> (o t) d") for b in range(2)]
                sp.wait_ge(added[1].sem, added[1].at(n, 4))
                for b, dst in enumerate(images):
                    sp.dma_start(dst[0:1], outb[HALF:HALF + 1, 2 * b, :]).then_inc(out_stored.sem, 16)
                    for a in range(2):
                        sp.dma_start(dst[1 + HALF * a:1 + HALF * (a + 1)],
                                     outb[0:HALF, 2 * b + a, :]).then_inc(out_stored.sem, 16)

            def body(i, nxt, load):
                max_rows(0, i, 0)
                max_rows(0, i, 1)
                if load is not None:
                    sp.wait_ge(patch_mm.sem, patch_mm.at(nxt, 4))
                    load_x(load)
                stack_parts(1, i)
                if nxt is not None:
                    stack_parts(0, nxt)
                max_rows(1, i, 0)
                max_rows(1, i, 1)
                store(i)

            for dst, src in LOADS:
                sp.dma_start(dst, src).then_inc(weights_in.sem, 16)
            sp.wait_ge(init_done.sem, init_done.at(0, N_INIT))
            sp.dma_start(gT[FC:FC + 2, 1, :], marks).then_inc(weights_in.sem, 16)
            load_x(0)
            sp.wait_ge(patch_mm.sem, patch_mm.at(0, 4))
            load_x(1)
            stack_parts(0, 0)
            body(0, 1, 2)
            with sp.Fori(1, PAIRS - 2) as i:
                body(i, sp.snap(i + 1), sp.snap(i + 2))
            body(PAIRS - 2, PAIRS - 1, None)
            body(PAIRS - 1, None, None)
            sp.wait_ge(out_stored.sem, out_stored.at(PAIRS - 1, out_stored.per))

        N_WEIGHTS = 16 * (len(LOADS) + 1)

        @block.gpsimd
        def _(pool):
            fills = [(xb[:, :, :, :], 1.0), (gT[:, :, :], 0.0), (V[0][:, :, :, :], 0.0), (V[1][:, :, :, :], 0.0),
                     (mx[:, :, :, :], 0.0), (comb[:, :, :], 1.0), (lg[:, :, :], 0.0), (ve[0][:, :, :], 1.0),
                     (ve[1][:, :, :], 1.0), (ve[2][:, :, :], 1.0), (half_s[:, :, :], -0.5),
                     (Ks[0][SR:SR + PARTS, :, :], 1.0), (Ks[1][SR:SR + PARTS, :, :], 1.0), (nT2[FC:FC + 1, :, :], 1.0),
                     (V[0][:, :, :, HD:HD + 1], 1.0), (V[1][:, :, :, HD:HD + 1], 1.0)]
            assert len(fills) == N_INIT
            for k, (dst, value) in enumerate(fills):
                pool.memset(dst, value).then_inc(init_done.sem, 1)
                pool.wait_ge(init_done.sem, k + 1)

            def rsqrt(which, n, tiles, used):
                t = tiles[0]
                if later(n):
                    pool.wait_ge(used.sem, used.at(n - 1, 4))
                pool.wait_ge(var_done[which].sem, var_done[which].at(n, t + 2))
                pool.tensor_tensor(rstd[which][:, t:t + 2, :], ve[which][:, t:t + 2, :], half_s[:, 0:2, :],
                                   ALU.pow).then_inc(rstd_done[which].sem, 1)

            def cut(s, n):
                for m in range(4):
                    pool.wait_ge(rest_done[s].sem, rest_done[s].at(n, m + 1))
                    hold_wait(pool)
                    pool.tensor_copy(parts[s][:, m, 1, :], rest[:, m, :]).then_inc(mid_done[s].sem, 1)
                    pool.wait_ge(mid_done[s].sem, mid_done[s].at(n, m + 1))
                    pool.tensor_tensor(parts[s][:, m, 2, :], rest[:, m, :], parts[s][:, m, 1, :],
                                       ALU.subtract).then_inc(lo_done[s].sem, 1)

            def body(i, nxt):
                if nxt is not None:
                    rsqrt(0, nxt, (0, 1), h0_normed)
                    rsqrt(0, nxt, (2, 3), h0_normed)
                rsqrt(2, i, (0, 1), n2_normed)
                rsqrt(2, i, (2, 3), n2_normed)
                if nxt is not None:
                    rsqrt(1, nxt, (0, 1), n1_normed)
                    rsqrt(1, nxt, (2, 3), n1_normed)
                cut(1, i)
                if nxt is not None:
                    cut(0, nxt)

            for which, used in ((0, h0_normed), (1, n1_normed)):
                for tiles in ((0, 1), (2, 3)):
                    rsqrt(which, 0, tiles, used)
            cut(0, 0)
            body(0, 1)
            with pool.Fori(1, PAIRS - 2) as i:
                body(i, i + 1)
            body(PAIRS - 2, PAIRS - 1)
            body(PAIRS - 1, None)

        @block.tensor
        def _(pe):
            def patch(n, tiles):
                for t in tiles:
                    b, a = divmod(t, 2)
                    pe.wait_ge(x_in.sem, x_in.at(n, x_in.per))
                    if t >= 2:
                        pe.wait_ge(h0_normed.sem, h0_normed.at(n, t - 1))
                    else:
                        if later(n):
                            pe.wait_ge(v_copied[0].sem, v_copied[0].at(n - 1, 4))
                    dst = ps[0:HALF, 6 + a, 0:D]
                    for q in range(QH):
                        k = 2 * XR + (q == 0)
                        mm = pe.matmul(dst, xb[0:k, b, 7 * a:7 * a + 7, q:q + PATCH * (GRID - 1) + 1:PATCH],
                                       w1_s[0:k, q, :], start=(q == 0), stop=(q == QH - 1))
                    mm.then_inc(patch_mm.sem, 1)

            def turn_h0(n):
                for a in range(2):
                    for b in range(2):
                        pe.wait_ge(h0_normed.sem, h0_normed.at(n, 2 * b + a + 1))
                        if b == 0:
                            pe.wait_ge(h0_normed.sem, h0_normed.at(n, 3 + a))
                        for c in range(2):
                            mm = pe.transpose(ps[0:FC, 6 + a, (2 * c + b) * HALF:(2 * c + b + 1) * HALF],
                                              h0n[:, 2 * b + a, c * FC:(c + 1) * FC], id_s[0:HALF, 0:HALF])
                    mm.then_inc(h0T_mm.sem, 1)

            def second(n):
                pe.wait_ge(gelu_done.sem, gelu_done.at(n, 4))
                for t in range(4):
                    b, a = divmod(t, 2)
                    if t >= 2:
                        pe.wait_ge(h1_copied.sem, h1_copied.at(n, t - 1))
                    dst = ps[0:ROWS[a], 6 + a, 0:D]
                    pe.matmul(dst, gT[0:FC, 0, tile_cols(t)], w2_s[0:FC, 0, :], start=True, stop=False)
                    pe.matmul(dst, gT[0:FC + 2, 1, tile_cols(t)], w2_s[0:FC + 2, 1, :],
                              start=False, stop=True).then_inc(w2_mm.sem, 1)

            def turn_n1(n):
                for t in range(4):
                    b, a = divmod(t, 2)
                    pe.wait_ge(n1_normed.sem, n1_normed.at(n, t + 1))
                    if t < 2:
                        pe.wait_ge(h1_copied.sem, h1_copied.at(n, t + 3))
                    else:
                        pe.wait_ge(n1T_copied.sem, n1T_copied.at(n, t - 1))
                    for c in range(2):
                        mm = pe.transpose(ps[0:FC, 6 + a, c * 128:c * 128 + ROWS[a]],
                                          n1[0:ROWS[a], t, c * FC:(c + 1) * FC], id_s[0:ROWS[a], 0:ROWS[a]])
                    mm.then_inc(n1T_mm.sem, 1)

            def qk(s, n):
                kr = [FC, FC] if s == 0 else [FC, FC + 1 + EXPERTS]
                nT = nT1 if s == 0 else nT2
                if s == 0:
                    pe.wait_ge(n1T_copied.sem, n1T_copied.at(n, 4))
                else:
                    pe.wait_ge(hwT_copied.sem, hwT_copied.at(n, 4))
                for m in range(4):
                    if s == 0:
                        if m >= 2:
                            pe.wait_ge(rest_done[0].sem, rest_done[0].at(n, m - 1))
                        dst = ps[0:FC, 6 + m % 2, 0:PT]
                    else:
                        dst = ps[0:FC, m, 0:PT]
                    for c in range(2):
                        mm = pe.matmul(dst, wqkv_s[s][0:kr[c], c, m * FC:(m + 1) * FC], nT[0:kr[c], c, :],
                                       start=(c == 0), stop=(s == 0 and c == 1))
                    if s == 1:
                        mm = pe.matmul(dst, wlora_s[:, m * FC:(m + 1) * FC], hwT[:, :], start=False, stop=True)
                    mm.then_inc(qk_mm[s].sem, 1)

            def values(s, n):
                kr = [FC, FC] if s == 0 else [FC, FC + 1 + EXPERTS]
                nT = nT1 if s == 0 else nT2
                for t in range(4):
                    b, a = divmod(t, 2)
                    if s == 0:
                        if t < 2:
                            pe.wait_ge(rest_done[0].sem, rest_done[0].at(n, t + 3))
                        else:
                            pe.wait_ge(v_copied[0].sem, v_copied[0].at(n, t - 1))
                        dst = ps[0:ROWS[a], 6 + a, 0:D]
                    else:
                        pe.wait_ge(rest_done[1].sem, rest_done[1].at(n, t + 1))
                        dst = ps[0:ROWS[a], t, 0:D]
                    pe.matmul(dst, nT[0:kr[0], 0, tile_cols(t)], wqkv_s[s][0:kr[0], 0, 2 * D:3 * D], start=True, stop=False)
                    mm = pe.matmul(dst, nT[0:kr[1], 1, tile_cols(t)], wqkv_s[s][0:kr[1], 1, 2 * D:3 * D],
                                   start=False, stop=(s == 0))
                    if s == 1:
                        mm = pe.matmul(dst, hwT[:, tile_cols(t)], wlora_s[:, 2 * D:3 * D], start=False, stop=True)
                    mm.then_inc(v_mm[s].sem, 1)

            def pass1(s, n, b):
                if b == 0:
                    pe.wait_ge(stacks_in[s].sem, stacks_in[s].at(n, stacks_in[s].per))
                    if s == 0:
                        if later(n):
                            pe.wait_ge(added[1].sem, added[1].at(n - 1, 4))
                    else:
                        pe.wait_ge(v_copied[1].sem, v_copied[1].at(n, 4))
                for a in range(2):
                    for g in range(GROUPS):
                        u = 6 * b + 3 * a + g
                        if u >= 2:
                            pe.wait_ge(max_done[s].sem, max_done[s].at(n, u - 1))
                        z, r = u % 2, ROWS[a]
                        keys = ROWS[0] if (s == 0 and a == 0) else TOK
                        for h in range(GH):
                            hd = GH * g + h
                            dst = ps[0:r, 2 * z + h // 2, (h % 2) * TOK:(h % 2) * TOK + keys]
                            mm = pe.matmul(dst, Qs[s][0:SR, hd, tile_cols(2 * b + a)],
                                           Ks[s][0:SR, hd, b * TOK:b * TOK + keys], start=True, stop=(s == 1))
                            if s == 0:
                                c0 = (h % 2) * TOK + a * ROWS[0]
                                mm = pe.matmul(ps[0:r, 2 * z + h // 2, c0:c0 + r], idb_s[0:r, 0:r],
                                               mask_s[0:r, a, 0:r], start=False, stop=True)
                        mm.then_inc(p1_mm[s].sem, 1)

            def turn_max(s, n, b):
                pe.wait_ge(max_parts[s].sem, max_parts[s].at(n, b + 1))
                if later(n):
                    pe.wait_ge(av_copied[s].sem, av_copied[s].at(n - 1, 6))
                if later(n):
                    pe.wait_ge(divided[s].sem, divided[s].at(n - 1, 3))
                if s == 1:
                    pe.wait_ge(hwT_copied.sem, hwT_copied.at(n, 4))
                else:
                    if later(n):
                        pe.wait_ge(divided[1].sem, divided[1].at(n - 1, 3))
                for a in range(2):
                    mm = pe.matmul(ps[0:PARTS * HEADS, 4 + b, a * ROWS[0]:a * ROWS[0] + ROWS[a]],
                                   mxp[0:ROWS[a], b, a, :, :].rearrange("p r h -> p (r h)"), idb_s[0:ROWS[a], 0:ROWS[a]],
                                   start=True, stop=True)
                mm.then_inc(mT_mm[s].sem, 1)

            def av(s, n, v):
                b, g = divmod(v, GROUPS)
                pe.wait_ge(exp_done[s].sem, exp_done[s].at(n, 2 * v + 2))
                if v >= 2:
                    pe.wait_ge(av_copied[s].sem, av_copied[s].at(n, v - 1))
                else:
                    pe.wait_ge(mT_copied[s].sem, mT_copied[s].at(n, 2))
                for a in range(2):
                    lo = ROWS[0] if (s == 0 and a == 1) else 0
                    for h in range(GH):
                        mm = pe.matmul(ps[32 * h:32 * h + 32, 4 + v % 2, lo:TOK],
                                       V[s][0:ROWS[a], 2 * b + a, GH * g + h, :],
                                       P[0:ROWS[a], (2 * v + a) % 4, h * TOK + lo:(h + 1) * TOK],
                                       start=(a == 0), stop=(a == 1))
                mm.then_inc(av_mm[s].sem, 1)

            def pass2(s, n, b):
                pe.wait_ge(mT_in[s][b].sem, mT_in[s][b].at(n, 16))
                if b == 0:
                    pe.wait_ge(v_copied[s].sem, v_copied[s].at(n, 4))
                for g in range(GROUPS):
                    v = 3 * b + g
                    for a in range(2):
                        u = 2 * v + a
                        if u >= 2:
                            pe.wait_ge(exp_done[s].sem, exp_done[s].at(n, u - 1))
                        else:
                            pe.wait_ge(max_done[s].sem, max_done[s].at(n, 12))
                        z, r = u % 2, ROWS[a]
                        lo = ROWS[0] if (s == 0 and a == 1) else 0
                        for h in range(GH):
                            hd = GH * g + h
                            c0 = (h % 2) * TOK
                            mm = pe.matmul(ps[0:r, 2 * z + h // 2, c0 + lo:c0 + TOK],
                                           Ks[s][0:SR + PARTS, hd, tile_cols(2 * b + a)],
                                           Qs[s][0:SR + PARTS, hd, b * TOK + lo:(b + 1) * TOK], start=True, stop=(s == 1))
                            if s == 0:
                                c0 += a * ROWS[0]
                                mm = pe.matmul(ps[0:r, 2 * z + h // 2, c0:c0 + r], idb_s[0:r, 0:r],
                                               mask_s[0:r, 2 + a, 0:r], start=False, stop=True)
                        mm.then_inc(p2_mm[s].sem, 1)
                    if v >= 1:
                        av(s, n, v - 1)
                if b == 1:
                    av(s, n, 2 * GROUPS - 1)

            def sums(s, n):
                for g in range(GROUPS):
                    pe.wait_ge(av_copied[s].sem, av_copied[s].at(n, 4 + g))
                    if g == 0:
                        pe.wait_ge(av_copied[s].sem, av_copied[s].at(n, 5))
                    if g == 1:
                        pe.wait_ge(av_copied[s].sem, av_copied[s].at(n, 6))
                    if g == 2:
                        pe.wait_ge(divided[s].sem, divided[s].at(n, 1))
                    pe.matmul(ps[:, 4 + g % 2, 0:PT], sel_s[:, :], O[:, g, :], start=True,
                              stop=True).then_inc(sum_mm[s].sem, 1)

            def project(s, n):
                pe.wait_ge(exp_done[s].sem, exp_done[s].at(n, 12))
                for t in range(4):
                    r = ROWS[t % 2]
                    for g in range(GROUPS):
                        if t == 0:
                            pe.wait_ge(divided[s].sem, divided[s].at(n, g + 1))
                        mm = pe.matmul(ps[0:r, t, 0:D], O[:, g, tile_cols(t)], wo_s[s][:, g, :],
                                       start=(g == 0), stop=(g == GROUPS - 1))
                    mm.then_inc(wo_mm[s].sem, 1)

            def turn_n2(n):
                for t in range(4):
                    r = ROWS[t % 2]
                    pe.wait_ge(n2_normed.sem, n2_normed.at(n, t + 1))
                    for c in range(2):
                        mm = pe.transpose(ps[0:FC, t, c * 128:c * 128 + r],
                                          n2[0:r, t, c * FC:(c + 1) * FC], id_s[0:r, 0:r])
                    mm.then_inc(n2T_mm.sem, 1)

            def gate(n):
                for t in range(4):
                    r = ROWS[t % 2]
                    pe.wait_ge(n2T_copied.sem, n2T_copied.at(n, t + 1))
                    dst = ps[0:r, t, 0:ER + EXPERTS]
                    pe.matmul(dst, nT2[0:FC, 0, tile_cols(t)], wgl_s[0:FC, 0, :], start=True, stop=False)
                    pe.matmul(dst, nT2[0:FC + 1, 1, tile_cols(t)], wgl_s[0:FC + 1, 1, :], start=False,
                              stop=True).then_inc(gate_mm.sem, 1)

            def turn_hw(n):
                for t in range(4):
                    r = ROWS[t % 2]
                    pe.wait_ge(hw_done.sem, hw_done.at(n, t + 1))
                    if t >= 2:
                        pe.wait_ge(hwT_copied.sem, hwT_copied.at(n, t - 1))
                    pe.transpose(ps[0:ER, 4 + t % 2, 0:r], hw[0:r, t, :], id_s[0:r, 0:r])
                    pe.transpose(ps[0:1 + EXPERTS, 4 + t % 2, 128:128 + r], comb[0:r, t, :],
                                 id_s[0:r, 0:r]).then_inc(hwT_mm.sem, 1)

            def body(i, nxt):
                pass1(0, i, 0)
                if nxt is not None:
                    patch(nxt, (0, 1))
                pass1(0, i, 1)
                if nxt is not None:
                    patch(nxt, (2, 3))
                turn_max(0, i, 0)
                turn_max(0, i, 1)
                pass2(0, i, 0)
                pass2(0, i, 1)
                sums(0, i)
                project(0, i)
                if nxt is not None:
                    turn_h0(nxt)
                turn_n2(i)
                gate(i)
                if nxt is not None:
                    second(nxt)
                turn_hw(i)
                qk(1, i)
                values(1, i)
                if nxt is not None:
                    turn_n1(nxt)
                    qk(0, nxt)
                    values(0, nxt)
                pass1(1, i, 0)
                pass1(1, i, 1)
                turn_max(1, i, 0)
                turn_max(1, i, 1)
                pass2(1, i, 0)
                pass2(1, i, 1)
                sums(1, i)
                project(1, i)

            pe.wait_ge(weights_in.sem, N_WEIGHTS)
            pe.wait_ge(init_done.sem, N_INIT)
            patch(0, (0, 1))
            patch(0, (2, 3))
            turn_h0(0)
            second(0)
            turn_n1(0)
            qk(0, 0)
            values(0, 0)
            body(0, 1)
            with pe.Fori(1, PAIRS - 2) as i:
                body(i, i + 1)
            body(PAIRS - 2, PAIRS - 1)
            body(PAIRS - 1, None)

        @block.scalar
        def _(act):
            def gelu(n):
                for a in range(2):
                    act.wait_ge(h0T_mm.sem, h0T_mm.at(n, a + 1))
                    if a == 0:
                        if later(n):
                            act.wait_ge(w2_mm.sem, w2_mm.at(n - 1, 4))
                    for c in range(2):
                        lo = a * ROWS[0]
                        dst = gT[0:FC, c, :].rearrange("p (b k) -> p b k", b=2)[:, :, lo:lo + HALF]
                        src = ps[0:FC, 6 + a, 2 * c * HALF:(2 * c + 2) * HALF].rearrange("p (b k) -> p b k", b=2)
                        nc.scalar.activation(dst, src, ACT.Gelu, bias=lnp_s[:, c, 1:2],
                                             scale=lnp_s[:, c, 0:1]).then_inc(gelu_done.sem, 1)

            def copy_h1(n):
                for t in range(4):
                    a = t % 2
                    act.wait_ge(w2_mm.sem, w2_mm.at(n, t + 1))
                    if t == 0:
                        if later(n):
                            act.wait_ge(added[0].sem, added[0].at(n - 1, 4))
                        if later(n):
                            act.wait_ge(n1_normed.sem, n1_normed.at(n - 1, 4))
                    nc.scalar.activation(h1[0:ROWS[a], t, :], ps[0:ROWS[a], 6 + a, 0:D],
                                         ACT.Copy).then_inc(h1_copied.sem, 1)

            def copy_nT1(n):
                for t in range(4):
                    a = t % 2
                    act.wait_ge(n1T_mm.sem, n1T_mm.at(n, t + 1))
                    if t == 0:
                        if later(n):
                            act.wait_ge(v_mm[0].sem, v_mm[0].at(n - 1, 4))
                    src = ps[0:FC, 6 + a, 0:256].rearrange("p (c k) -> p c k", c=2)[:, :, 0:ROWS[a]]
                    nc.scalar.activation(nT1[:, :, tile_cols(t)], src, ACT.Copy).then_inc(n1T_copied.sem, 1)

            def high(s, n):
                if later(n):
                    act.wait_ge(parts_out[s].sem, parts_out[s].at(n - 1, 4 * 16))
                for m in range(4):
                    act.wait_ge(qk_mm[s].sem, qk_mm[s].at(n, m + 1))
                    bank = 6 + m % 2 if s == 0 else m
                    nc.scalar.activation(parts[s][:, m, 0, :], ps[0:FC, bank, 0:PT], ACT.Copy).then_inc(hi_done[s].sem, 1)

            def copy_v(s, n):
                for t in range(4):
                    a = t % 2
                    act.wait_ge(v_mm[s].sem, v_mm[s].at(n, t + 1))
                    if t == 0:
                        if later(n):
                            act.wait_ge(av_mm[s].sem, av_mm[s].at(n - 1, 6))
                    bank = 6 + a if s == 0 else t
                    nc.scalar.activation(V[s][0:ROWS[a], t, :, 0:HD],
                                         ps[0:ROWS[a], bank, 0:D].rearrange("p (h d) -> p h d", d=HD),
                                         ACT.Copy).then_inc(v_copied[s].sem, 1)

            def copy_mT(s, n):
                for b in range(2):
                    act.wait_ge(mT_mm[s].sem, mT_mm[s].at(n, b + 1))
                    if b == 0:
                        if s == 0:
                            if later(n):
                                act.wait_ge(mT_out[1].sem, mT_out[1].at(n - 1, 32))
                        else:
                            act.wait_ge(mT_out[0].sem, mT_out[0].at(n, 32))
                    nc.scalar.activation(mT[:, b, :], ps[0:PARTS * HEADS, 4 + b, 0:TOK],
                                         ACT.Copy).then_inc(mT_copied[s].sem, 1)

            def copy_av(s, n, v):
                b, g = divmod(v, GROUPS)
                act.wait_ge(av_mm[s].sem, av_mm[s].at(n, v + 1))
                if v == 0:
                    if s == 0:
                        if later(n):
                            act.wait_ge(wo_mm[1].sem, wo_mm[1].at(n - 1, 4))
                    else:
                        act.wait_ge(wo_mm[0].sem, wo_mm[0].at(n, 4))
                nc.scalar.activation(O[:, g, b * TOK:(b + 1) * TOK], ps[:, 4 + v % 2, 0:TOK],
                                     ACT.Copy).then_inc(av_copied[s].sem, 1)

            def exps(s, n):
                for u in range(12):
                    a = u % 2
                    act.wait_ge(p2_mm[s].sem, p2_mm[s].at(n, u + 1))
                    if u >= 4:
                        act.wait_ge(av_mm[s].sem, av_mm[s].at(n, u // 2 - 1))
                    lo = ROWS[0] if (s == 0 and a == 1) else 0
                    dst = P[0:ROWS[a], u % 4, :].rearrange("p (k h c) -> p k h c", k=2, h=2)[:, :, :, lo:TOK]
                    nc.scalar.activation(dst, score_slot(u % 2, ROWS[a], lo, TOK - lo), ACT.Exp,
                                         scale=SCALE).then_inc(exp_done[s].sem, 1)
                    if a == 1 and u >= 3:
                        copy_av(s, n, u // 2 - 1)
                copy_av(s, n, 5)

            def copy_nT2(n):
                for t in range(4):
                    a = t % 2
                    act.wait_ge(n2T_mm.sem, n2T_mm.at(n, t + 1))
                    if t == 0:
                        if later(n):
                            act.wait_ge(v_mm[1].sem, v_mm[1].at(n - 1, 4))
                    src = ps[0:FC, t, 0:256].rearrange("p (c k) -> p c k", c=2)[:, :, 0:ROWS[a]]
                    nc.scalar.activation(nT2[0:FC, :, tile_cols(t)], src, ACT.Copy).then_inc(n2T_copied.sem, 1)

            def copy_hwT(n):
                for t in range(4):
                    a = t % 2
                    act.wait_ge(hwT_mm.sem, hwT_mm.at(n, t + 1))
                    nc.scalar.activation(hwT[:, tile_cols(t)], ps[0:ER, 4 + a, 0:ROWS[a]], ACT.Copy)
                    nc.scalar.activation(nT2[FC:FC + 1 + EXPERTS, 1, tile_cols(t)],
                                         ps[0:1 + EXPERTS, 4 + a, 128:128 + ROWS[a]], ACT.Copy).then_inc(hwT_copied.sem, 1)

            def body(i, nxt):
                copy_mT(0, i)
                exps(0, i)
                if nxt is not None:
                    gelu(nxt)
                copy_nT2(i)
                if nxt is not None:
                    copy_h1(nxt)
                act.wait_ge(logits_done.sem, logits_done.at(i, 1))
                nc.scalar.activation(pe_[:, :, :], lg[:, :, :], ACT.Exp).then_inc(gate_exp.sem, 1)
                copy_hwT(i)
                high(1, i)
                copy_v(1, i)
                if nxt is not None:
                    copy_nT1(nxt)
                    high(0, nxt)
                    copy_v(0, nxt)
                copy_mT(1, i)
                exps(1, i)

            act.wait_ge(weights_in.sem, N_WEIGHTS)
            act.wait_ge(init_done.sem, N_INIT)
            gelu(0)
            copy_h1(0)
            copy_nT1(0)
            high(0, 0)
            copy_v(0, 0)
            body(0, 1)
            with act.Fori(1, PAIRS - 2) as i:
                body(i, i + 1)
            body(PAIRS - 2, PAIRS - 1)
            body(PAIRS - 1, None)

        @block.vector
        def _(dve):
            at = {}

            def reset():
                for chain in (dve_here, *dve_stats):
                    at[chain] = 0

            def link(chain, n, ins):
                ins.then_inc(chain.sem, 1)
                at[chain] += 1
                dve.wait_ge(chain.sem, chain.at(n, at[chain]))

            def moments(which, n, src, r, t):
                link(dve_stats[which], n, dve.bn_stats(st[which][0:r, t, :], src))
                hold_wait(dve)
                link(dve_stats[which], n, dve.bn_aggr(mv[which][0:r, t, :], st[which][0:r, t, :]))
                dve.tensor_scalar(ve[which][0:r, t, :], mv[which][0:r, t, 1:2], EPS, None,
                                  ALU.add).then_inc(var_done[which].sem, 1)

            def scale(which, n, dst, src, r, t, done):
                dve.wait_ge(rstd_done[which].sem, rstd_done[which].at(n, t // 2 + 1))
                dve.tensor_scalar(dst, src, mv[which][0:r, t, 0:1], rstd[which][0:r, t, :],
                                  ALU.subtract, ALU.mult).then_inc(done.sem, 1)

            def norm_h0(n, tiles):
                for t in tiles:
                    dve.wait_ge(patch_mm.sem, patch_mm.at(n, t + 1))
                    moments(0, n, ps[0:HALF, 6 + t % 2, 0:D], HALF, t)
                for t in tiles:
                    if t == 0:
                        if later(n):
                            dve.wait_ge(h0T_mm.sem, h0T_mm.at(n - 1, 2))
                    scale(0, n, h0n[:, t, :], ps[0:HALF, 6 + t % 2, 0:D], HALF, t, h0_normed)

            def norm_n1(n):
                for tiles in ((0, 1), (2, 3)):
                    for t in tiles:
                        dve.wait_ge(h1_copied.sem, h1_copied.at(n, t + 1))
                        moments(1, n, h1[0:ROWS[t % 2], t, :], ROWS[t % 2], t)
                    for t in tiles:
                        if t == 0:
                            if later(n):
                                dve.wait_ge(n1T_mm.sem, n1T_mm.at(n - 1, 4))
                        r = ROWS[t % 2]
                        scale(1, n, n1[0:r, t, :], h1[0:r, t, :], r, t, n1_normed)

            def remainder(s, n):
                for m in range(4):
                    dve.wait_ge(hi_done[s].sem, hi_done[s].at(n, m + 1))
                    if s == 0:
                        if later(n):
                            dve.wait_ge(lo_done[1].sem, lo_done[1].at(n - 1, m + 1))
                    else:
                        dve.wait_ge(lo_done[0].sem, lo_done[0].at(n, m + 1))
                    bank = 6 + m % 2 if s == 0 else m
                    dve.tensor_tensor(rest[:, m, :], ps[0:FC, bank, 0:PT], parts[s][:, m, 0, :],
                                      ALU.subtract).then_inc(rest_done[s].sem, 1)

            def maxima(s, n, b):
                for a in range(2):
                    for g in range(GROUPS):
                        u = 6 * b + 3 * a + g
                        keys = ROWS[0] if (s == 0 and a == 0) else TOK
                        dve.wait_ge(p1_mm[s].sem, p1_mm[s].at(n, u + 1))
                        dve.tensor_reduce(mx[0:ROWS[a], b, a, GH * g:GH * (g + 1)].rearrange("p (k h) -> p k h", k=2),
                                          score_slot(u % 2, ROWS[a], 0, keys), AX_X,
                                          ALU.max).then_inc(max_done[s].sem, 1)
                dve.wait_ge(max_done[s].sem, max_done[s].at(n, 6 * b + 6))
                if s == 0:
                    if later(n):
                        dve.wait_ge(mT_mm[1].sem, mT_mm[1].at(n - 1, 2))
                else:
                    dve.wait_ge(mT_mm[0].sem, mT_mm[0].at(n, 2))
                m, p = mx[:, b], mxp[:, b]
                link(dve_here, n, dve.tensor_scalar(p[:, :, 0, :], m, -1.0, None, ALU.mult))
                link(dve_here, n, dve.scalar_tensor_tensor(out=mxr[:, :, :], in0=m, scalar=-1.0, in1=p[:, :, 0, :],
                                                           op0=ALU.mult, op1=ALU.subtract))
                link(dve_here, n, dve.tensor_copy(p[:, :, 1, :], mxr[:, :, :]))
                dve.tensor_tensor(p[:, :, 2, :], mxr[:, :, :], p[:, :, 1, :], ALU.subtract).then_inc(max_parts[s].sem, 1)

            def divide(s, n):
                for g in range(GROUPS):
                    dve.wait_ge(sum_mm[s].sem, sum_mm[s].at(n, g + 1))
                    link(dve_here, n, dve.reciprocal(inv[:, :], ps[:, 4 + g % 2, 0:PT]))
                    dve.tensor_tensor(O[:, g, :], O[:, g, :], inv[:, :], ALU.mult).then_inc(divided[s].sem, 1)
                    dve.wait_ge(divided[s].sem, divided[s].at(n, g + 1))

            def add(s, n):
                res, dst = (h1, h2) if s == 0 else (h2, outb)
                if s == 1:
                    if later(n):
                        dve.wait_ge(out_stored.sem, out_stored.at(n - 1, out_stored.per))
                for t in range(4):
                    r = ROWS[t % 2]
                    dve.wait_ge(wo_mm[s].sem, wo_mm[s].at(n, t + 1))
                    dve.tensor_tensor(dst[0:r, t, :], ps[0:r, t, 0:D], res[0:r, t, :], ALU.add).then_inc(added[s].sem, 1)

            def norm_n2(n):
                for tiles in ((0, 1), (2, 3)):
                    for t in tiles:
                        dve.wait_ge(added[0].sem, added[0].at(n, t + 1))
                        moments(2, n, h2[0:ROWS[t % 2], t, :], ROWS[t % 2], t)
                    for t in tiles:
                        if t == 0:
                            if later(n):
                                dve.wait_ge(n2T_mm.sem, n2T_mm.at(n - 1, 4))
                        r = ROWS[t % 2]
                        scale(2, n, n2[0:r, t, :], h2[0:r, t, :], r, t, n2_normed)

            def choose(n):
                def bc(ap):
                    return ap.to_broadcast([HALF + 1, 4, EXPERTS])

                rk = rank_s[:, :].unsqueeze(1).to_broadcast([HALF + 1, 4, EXPERTS])
                dve.wait_ge(gate_mm.sem, gate_mm.at(n, 4))
                for a in range(2):
                    r = ROWS[a]
                    logits = ps[0:r, a:4:2, ER:ER + EXPERTS]
                    link(dve_here, n, dve.tensor_reduce(gm[0:r, a:4:2, 0], logits, AX_X, ALU.max))
                    ins = dve.tensor_tensor(lg[0:r, a:4:2, :], logits,
                                            gm[0:r, a:4:2, :].to_broadcast([r, 2, EXPERTS]), ALU.subtract)
                    if a == 0:
                        link(dve_here, n, ins)
                    else:
                        ins.then_inc(logits_done.sem, 1)
                dve.wait_ge(gate_exp.sem, gate_exp.at(n, 1))
                link(dve_here, n, dve.tensor_reduce(gm[:, :, 0], pe_[:, :, :], AX_X, ALU.add))
                link(dve_here, n, dve.reciprocal(gm[:, :, :], gm[:, :, :]))
                link(dve_here, n, dve.tensor_tensor(pr[:, :, :], pe_[:, :, :], bc(gm[:, :, :]), ALU.mult))
                src = pr
                for sel_k in (s1, s2):
                    link(dve_here, n, dve.tensor_reduce(gm[:, :, 0], src[:, :, :], AX_X, ALU.max))
                    link(dve_here, n, dve.tensor_tensor(ge[:, :, :], src[:, :, :], bc(gm[:, :, :]), ALU.is_equal))
                    link(dve_here, n, dve.tensor_tensor(gc[:, :, :], ge[:, :, :], rk, ALU.mult))
                    link(dve_here, n, dve.tensor_reduce(gm[:, :, 0], gc[:, :, :], AX_X, ALU.max))
                    link(dve_here, n, dve.tensor_tensor(sel_k[:, :, :], gc[:, :, :], bc(gm[:, :, :]), ALU.is_equal))
                    if sel_k is s1:
                        link(dve_here, n, dve.scalar_tensor_tensor(out=pe_[:, :, :], in0=s1[:, :, :], scalar=-BIG,
                                                                   in1=pr[:, :, :], op0=ALU.mult, op1=ALU.add))
                        src = pe_
                    else:
                        link(dve_here, n, dve.tensor_tensor(ge[:, :, :], s1[:, :, :], s2[:, :, :], ALU.add))
                dve.scalar_tensor_tensor(out=comb[:, :, 1:1 + EXPERTS], in0=ge[:, :, :], scalar=LORA_SCALE,
                                         in1=pr[:, :, :], op0=ALU.mult, op1=ALU.mult).then_inc(comb_done.sem, 1)
                dve.wait_ge(comb_done.sem, comb_done.at(n, 1))
                for t in range(4):
                    r = ROWS[t % 2]
                    dve.tensor_tensor(hw[0:r, t, :].rearrange("p (e k) -> p e k", e=EXPERTS),
                                      ps[0:r, t, 0:ER].rearrange("p (e k) -> p e k", e=EXPERTS),
                                      comb[0:r, t, 1:1 + EXPERTS].unsqueeze(2).to_broadcast([r, EXPERTS, RANK]),
                                      ALU.mult).then_inc(hw_done.sem, 1)

            def body(i, nxt):
                reset()
                maxima(0, i, 0)
                if nxt is not None:
                    norm_h0(nxt, (0, 1))
                maxima(0, i, 1)
                if nxt is not None:
                    norm_h0(nxt, (2, 3))
                divide(0, i)
                add(0, i)
                norm_n2(i)
                choose(i)
                if nxt is not None:
                    norm_n1(nxt)
                remainder(1, i)
                if nxt is not None:
                    remainder(0, nxt)
                maxima(1, i, 0)
                maxima(1, i, 1)
                divide(1, i)
                add(1, i)
                assert at[dve_here] == dve_here.per, at[dve_here]

            dve.wait_ge(weights_in.sem, N_WEIGHTS)
            dve.wait_ge(init_done.sem, N_INIT)
            reset()
            norm_h0(0, (0, 1))
            norm_h0(0, (2, 3))
            norm_n1(0)
            remainder(0, 0)
            body(0, 1)
            with dve.Fori(1, PAIRS - 2) as i:
                body(i, i + 1)
            body(PAIRS - 2, PAIRS - 1)
            body(PAIRS - 1, None)


def kernel(x, cls_tok, L0_tok_W1, L0_tok_b1, L0_tok_ln_w, L0_tok_ln_b, L0_tok_W2, L0_tok_b2,
           L0_attn_wq, L0_attn_wk, L0_attn_wv, L0_attn_wo, L0_ffn_Wg, L0_ffn_bg, L0_ffn_Wqkv, L0_ffn_bqkv,
           L0_ffn_Wproj, L0_ffn_bproj, L0_ffn_A, L0_ffn_ba, L0_ffn_Bm, L0_ffn_bb):
    import numpy as np
    import concourse.bacc as bacc
    from concourse.bass_utils import run_bass_kernel_spmd

    f = np.float32

    def zeros(*shape):
        return np.zeros(shape, f)

    order = np.array([(6 * m + h) * HD + j for m in range(2) for j in range(HD) for h in range(6)])

    def qkv_cols(wt):
        return np.concatenate([wt[:, 0:D][:, order], wt[:, D:2 * D][:, order], wt[:, 2 * D:]], axis=1)

    w1 = zeros(2 * XR + 1, QH, D)
    for s in range(2):
        w1[XR * s:XR * (s + 1)] = L0_tok_W1.reshape(XR, PATCH, D)[:, QH * s:QH * (s + 1)]
    w1[2 * XR, 0] = L0_tok_b1
    w2 = zeros(FC + 2, 2, D)
    w2[0:FC, 0], w2[0:FC, 1] = L0_tok_W2[0:FC], L0_tok_W2[FC:D]
    w2[FC, 1], w2[FC + 1, 1] = L0_tok_b2, cls_tok[0, 0]
    lnp = np.stack([L0_tok_ln_w.reshape(2, FC).T, L0_tok_ln_b.reshape(2, FC).T], axis=2)
    wq1 = qkv_cols(np.concatenate([L0_attn_wq.T, L0_attn_wk.T, L0_attn_wv.T], axis=1))
    wqkv1 = wq1.reshape(2, FC, 3 * D).transpose(1, 0, 2)
    wq2 = qkv_cols(L0_ffn_Wqkv.T)
    wqkv2 = zeros(FC + 1 + EXPERTS, 2, 3 * D)
    wqkv2[0:FC] = wq2.reshape(2, FC, 3 * D).transpose(1, 0, 2)
    wqkv2[FC, 1] = qkv_cols(L0_ffn_bqkv[None])[0]
    wqkv2[FC + 1:, 1] = qkv_cols(L0_ffn_bb)
    wlora = qkv_cols(L0_ffn_Bm.transpose(0, 2, 1).reshape(ER, 3 * D))
    wgl = zeros(FC + 1, 2, ER + EXPERTS)
    wgl[0:FC, :, 0:ER] = L0_ffn_A.reshape(ER, D).T.reshape(2, FC, ER).transpose(1, 0, 2)
    wgl[0:FC, :, ER:] = L0_ffn_Wg.T.reshape(2, FC, EXPERTS).transpose(1, 0, 2)
    wgl[FC, 1, 0:ER], wgl[FC, 1, ER:] = L0_ffn_ba.reshape(ER), L0_ffn_bg

    def wo_rows(wt):
        r = zeros(GH, 32, GROUPS, D)
        r[:, 0:HD] = wt.reshape(GROUPS, GH, HD, D).transpose(1, 2, 0, 3)
        return r.reshape(128, GROUPS, D)

    wo1, wo2 = wo_rows(L0_attn_wo.T), wo_rows(L0_ffn_Wproj.T)
    wo2[HD, 0] = L0_ffn_bproj

    ident = np.eye(128, dtype=f)
    bf = mybir.dt.np(BF16) if hasattr(mybir.dt, "np") else __import__("ml_dtypes").bfloat16
    seq = [np.array(list(range(1, HALF + 1)) + [0]), np.arange(HALF)]
    masks = np.zeros((HALF + 1, 4, HALF + 1), f)
    for a in range(2):
        r = ROWS[a]
        late = np.where(seq[a][None, :] > seq[a][:, None], f(-1e9), f(0))
        masks[0:r, a, 0:r] = late
        masks[0:r, 2 + a, 0:r] = late.T
    sel = zeros(128, 128)
    for h in range(GH):
        sel[32 * h + HD, 32 * h:32 * h + 32] = 1
    marks = np.ones((2, PT), f)
    for b in range(2):
        marks[0, b * TOK + HALF] = 0
    marks[1] = 1 - marks[0]
    rank8 = np.tile(np.arange(EXPERTS, 0, -1, dtype=f), (HALF + 1, 1))

    arrays = dict(x=x, w1=w1, w2=w2, lnp=lnp, wqkv1=wqkv1, wo1=wo1, wgl=wgl, wqkv2=wqkv2, wlora=wlora, wo2=wo2,
                  ident=ident, identb=ident.astype(bf), masks=masks.astype(bf), sel=sel, marks=marks, rank8=rank8)
    nc = bacc.Bacc("TRN2", target_bir_lowering=False, num_devices=1)
    named, args = {}, []
    for name, a in arrays.items():
        a = np.ascontiguousarray(a)
        named[f"in_{name}"] = a
        args.append(nc.dram_tensor(f"in_{name}", a.shape, mybir.dt.from_np(a.dtype), kind="ExternalInput").ap())
    out = nc.dram_tensor("out_0", (IMAGES, TOK, D), F32, kind="ExternalOutput").ap()
    vit_tower(nc, *args, out)
    r = run_bass_kernel_spmd(nc, [named], core_ids=[0])
    return r.results[0]["out_0"]
```

```python
from contextlib import ExitStack

import concourse.bass as bass
from concourse import mybir

F32 = mybir.dt.float32
BF16 = mybir.dt.bfloat16
ALU = mybir.AluOpType
ACT = mybir.ActivationFunctionType
AX_X = mybir.AxisListType.X

IMAGES, CHANNELS, IMG = 128, 3, 224
PATCH = 16
GRID = IMG // PATCH
D = 192
HEADS, HD = 12, 16
TOK = GRID * GRID + 1
HALF = GRID * GRID // 2
ROWS = [HALF + 1, HALF]
PAIRS = IMAGES // 2
PT = 2 * TOK
FC = D // 2
QH = PATCH // 2
XR = CHANNELS * PATCH
EXPERTS, RANK = 8, 16
ER = EXPERTS * RANK
GH = 4
GROUPS = HEADS // GH
PARTS = 3
SR = 6 * HD
EPS = 1e-5
SCALE = float(HD) ** -0.5
LORA_SCALE = 2.0
BIG = 3e38

Q_RUNS = [(0, 0, 1), (1, 0, 1), (2, 0, 1), (3, 1, 1), (4, 1, 2)]
K_RUNS = [(0, 0, 3), (3, 0, 2), (5, 0, 1)]


class Count:

    def __init__(self, ctx, nc, name, per):
        self.sem = ctx.enter_context(nc.semaphore(name))
        self.per = per

    def at(self, pair, k):
        return pair * self.per + k


def later(pair):
    return not (isinstance(pair, int) and pair == 0)


def tile_cols(t):
    b, a = divmod(t, 2)
    c = b * TOK + a * (HALF + 1)
    return slice(c, c + ROWS[a])


def vit_tower(nc, x, w1, w2, lnp, wqkv1, wo1, wgl, wqkv2, wlora, wo2, ident, identb, masks, sel, marks, rank8, out):
    with ExitStack() as ctx:
        def sb(name, shape, dt=F32):
            return ctx.enter_context(nc.sbuf_tensor(name, shape, dt))

        def cnt(name, per):
            return Count(ctx, nc, name, per)

        def cnt2(name, per):
            return [Count(ctx, nc, f"{name}{s}", per) for s in range(2)]

        ps = ctx.enter_context(nc.psum_tensor("ps", [128, 8, 512], F32))
        dparts = [nc.dram_tensor(f"parts_dram{s}", (2, 2, PARTS, FC, PT), BF16, kind="Internal").ap() for s in range(2)]
        dmax = [nc.dram_tensor(f"max_dram{s}", (2, PARTS * HEADS, TOK), BF16, kind="Internal").ap() for s in range(2)]

        w1_s = sb("w1_s", [XR * 2 + 1, QH, D])
        w2_s = sb("w2_s", [FC + 2, 2, D])
        lnp_s = sb("lnp_s", [FC, 2, 2])
        wqkv_s = [sb("wqkv1_s", [FC, 2, 3 * D]), sb("wqkv2_s", [FC + 1 + EXPERTS, 2, 3 * D])]
        wlora_s = sb("wlora_s", [ER, 3 * D])
        wgl_s = sb("wgl_s", [FC + 1, 2, ER + EXPERTS])
        wo_s = [sb("wo1_s", [128, GROUPS, D]), sb("wo2_s", [128, GROUPS, D])]
        id_s = sb("id_s", [128, 128])
        idb_s = sb("idb_s", [128, 128], BF16)
        mask_s = sb("mask_s", [HALF + 1, 4, HALF + 1], BF16)
        sel_s = sb("sel_s", [128, 128])
        rank_s = sb("rank_s", [HALF + 1, EXPERTS])
        xb = sb("xb", [XR * 2 + 1, 2, GRID, IMG])
        h0n = sb("h0n", [HALF, 4, D])
        gT = sb("gT", [FC + 2, 2, PT])
        h1 = sb("h1", [HALF + 1, 4, D])
        h1k = sb("h1k", [HALF + 1, 4, D])
        n1 = sb("n1", [HALF + 1, 4, D])
        nT1 = sb("nT1", [FC, 2, PT])
        h2 = sb("h2", [HALF + 1, 4, D])
        n2 = sb("n2", [HALF + 1, 4, D])
        nT2 = sb("nT2", [FC + 1 + EXPERTS, 2, PT + 1])
        hw = sb("hw", [HALF + 1, 4, ER])
        hwT = sb("hwT", [ER, PT])
        outb = sb("outb", [HALF + 1, 4, D])
        st = [sb(f"st{k}", [HALF + 1, 4, 6]) for k in range(3)]
        mv = [sb(f"mv{k}", [HALF + 1, 4, 2]) for k in range(3)]
        ve = [sb(f"ve{k}", [HALF + 1, 4, 1]) for k in range(3)]
        half_s = sb("half_s", [HALF + 1, 2, 1])
        rstd = [sb(f"rstd{k}", [HALF + 1, 4, 1]) for k in range(3)]
        parts = [sb(f"parts{s}", [FC, 4, PARTS, PT], BF16) for s in range(2)]
        rest = sb("rest", [FC, 4, PT])
        Qs = [sb(f"Qs{s}", [SR + PARTS, HEADS, PT], BF16) for s in range(2)]
        Ks = [sb(f"Ks{s}", [SR + PARTS, HEADS, PT], BF16) for s in range(2)]
        V = [sb(f"V{s}", [128, 4, HEADS, 32]) for s in range(2)]
        mx = sb("mx", [HALF + 1, 2, 2, HEADS])
        mxr = sb("mxr", [HALF + 1, 2, HEADS])
        mxp = sb("mxp", [HALF + 1, 2, 2, PARTS, HEADS], BF16)
        mT = sb("mT", [PARTS * HEADS, 2, TOK], BF16)
        P = sb("P", [128, 4, GH * TOK])
        O = [sb(f"O{s}", [128, GROUPS, PT]) for s in range(2)]
        inv = sb("inv", [128, PT])
        lg = sb("lg", [HALF + 1, 4, EXPERTS])
        pe_ = sb("probs", [HALF + 1, 4, EXPERTS])
        pr = sb("pr", [HALF + 1, 4, EXPERTS])
        ge = sb("ge", [HALF + 1, 4, EXPERTS])
        gs = sb("gs", [HALF + 1, 4, ER + EXPERTS])
        gc = sb("gc", [HALF + 1, 4, EXPERTS])
        s1 = sb("s1", [HALF + 1, 4, EXPERTS])
        s2 = sb("s2", [HALF + 1, 4, EXPERTS])
        gm = sb("gm", [HALF + 1, 4, 1])
        gsum = sb("gsum", [HALF + 1, 4, 1])
        comb = sb("comb", [HALF + 1, 4, 1 + EXPERTS])

        weights_in = cnt("weights_in", 0)
        init_done = cnt("init_done", 0)
        wait_held = cnt("wait_held", 0)
        x_in = cnt("x_in", 12 * 16)
        patch_mm = cnt("patch_mm", 4)
        h0_normed = cnt("h0_normed", 4)
        h0T_mm = cnt("h0T_mm", 2)
        gelu_done = cnt("gelu_done", 4)
        w2_mm = cnt("w2_mm", 4)
        h1_copied = cnt("h1_copied", 4)
        n1_normed = cnt("n1_normed", 4)
        n1T_mm = cnt("n1T_mm", 4)
        n1T_copied = cnt("n1T_copied", 4)
        qk_mm = cnt2("qk_mm", 4)
        hi_done = cnt2("hi_done", 4)
        rest_done = cnt2("rest_done", 4)
        lo_done = cnt2("lo_done", 4)
        mid_done = cnt2("mid_done", 4)
        parts_out = cnt2("parts_out", 4 * 16)
        stacks_in = cnt2("stacks_in", 8 * 16)
        v_mm = cnt2("v_mm", 4)
        v_copied = cnt2("v_copied", 4)
        p1_mm = cnt2("p1_mm", 12)
        max_done = cnt2("max_done", 12)
        max_parts = cnt2("max_parts", 2)
        mT_mm = cnt2("mT_mm", 2)
        mT_copied = cnt2("mT_copied", 2)
        mT_out = cnt2("mT_out", 2 * 16)
        mT_in = [[cnt(f"mT_in{s}{b}", 16) for b in range(2)] for s in range(2)]
        p2_mm = cnt2("p2_mm", 12)
        exp_done = cnt2("exp_done", 12)
        av_mm = cnt2("av_mm", 6)
        av_copied = cnt2("av_copied", 6)
        sum_mm = cnt2("sum_mm", 3)
        divided = cnt2("divided", 3)
        wo_mm = cnt2("wo_mm", 4)
        added = cnt2("added", 4)
        n2_normed = cnt("n2_normed", 4)
        n2T_mm = cnt("n2T_mm", 4)
        n2T_copied = cnt("n2T_copied", 4)
        gate_mm = cnt("gate_mm", 4)
        gate_copied = cnt("gate_copied", 2)
        kept = cnt("kept", 1)
        logits_done = cnt("logits_done", 1)
        gate_exp = cnt("gate_exp", 1)
        comb_done = cnt("comb_done", 1)
        hw_done = cnt("hw_done", 1)
        hwT_mm = cnt("hwT_mm", 4)
        hwT_copied = cnt("hwT_copied", 4)
        out_stored = cnt("out_stored", 6 * 16)
        dve_stats = [cnt(f"dve_stats{k}", 8) for k in range(3)]
        dve_here = cnt("dve_here", 12)
        dve_max = cnt2("dve_max", 2 * 3)
        dve_div = cnt2("dve_div", GROUPS)
        var_done = [cnt(f"var_done{k}", 4) for k in range(3)]
        rstd_done = [cnt(f"rstd_done{k}", 2) for k in range(3)]

        LOADS = [(w1_s[:, :, :], w1), (w2_s[:, :, :], w2), (lnp_s[:, :, :], lnp), (wqkv_s[0][:, :, :], wqkv1),
                 (wo_s[0][:, :, :], wo1), (wgl_s[:, :, :], wgl), (wqkv_s[1][:, :, :], wqkv2), (wlora_s[:, :], wlora),
                 (wo_s[1][:, :, :], wo2), (id_s[:, :], ident), (idb_s[:, :], identb), (mask_s[:, :, :], masks),
                 (sel_s[:, :], sel), (rank_s[:, :], rank8)]
        N_INIT = 18

        def score_slot(z, n, lo, cols):
            return ps[0:n, 2 * z:2 * z + 2, 0:2 * TOK].rearrange("p k (h c) -> p k h c", h=2)[:, :, :, lo:lo + cols]

        block = ctx.enter_context(nc.Block())

        def hold_wait(eng):
            eng.sem_inc(wait_held.sem, 1)

        @block.sync
        def _(sp):
            def load_x(n):
                img = x.rearrange("b c (g p) w -> b c p g w", p=PATCH)
                for b in range(2):
                    for c in range(CHANNELS):
                        for s in range(2):
                            r = XR * s + PATCH * c
                            src = img[bass.ds(2 * n + b, 1), c].rearrange("o p g w -> (o p) g w")
                            sp.dma_start(xb[r:r + PATCH, b, :, 0:IMG - QH * s],
                                         src[:, :, QH * s:IMG]).then_inc(x_in.sem, 16)

            def stack_parts(s, n):
                if later(n):
                    sp.wait_ge(stacks_in[s].sem, stacks_in[s].at(n - 1, stacks_in[s].per))
                hold_wait(sp)
                for m in range(4):
                    sp.wait_ge(lo_done[s].sem, lo_done[s].at(n, m + 1))
                    sp.dma_start(dparts[s][m // 2, m % 2].rearrange("r p c -> p r c"),
                                 parts[s][:, m, :, :]).then_inc(parts_out[s].sem, 16)
                sp.wait_ge(parts_out[s].sem, parts_out[s].at(n, 4 * 16))
                if later(n):
                    sp.wait_ge(p2_mm[s].sem, p2_mm[s].at(n - 1, 12))
                for qk, (stack, runs) in enumerate(((Qs[s], Q_RUNS), (Ks[s], K_RUNS))):
                    for slot, part, k in runs:
                        src = dparts[s][qk].rearrange("m r (j h) c -> (r j) m h c", h=6)
                        sp.dma_start(stack[HD * slot:HD * (slot + k), :, :].rearrange("p (m h) c -> p m (h c)", m=2),
                                     src[HD * part:HD * (part + k)].rearrange("p m h c -> p m (h c)")).then_inc(stacks_in[s].sem, 16)

            def max_rows(s, n, b):
                sp.wait_ge(mT_copied[s].sem, mT_copied[s].at(n, b + 1))
                sp.dma_start(dmax[s][b], mT[:, b, :]).then_inc(mT_out[s].sem, 16)
                sp.wait_ge(mT_out[s].sem, mT_out[s].at(n, 16 * (b + 1)))
                sp.dma_start(Qs[s][SR:SR + PARTS, :, b * TOK:(b + 1) * TOK],
                             dmax[s][b].rearrange("(r h) c -> r h c", r=PARTS)).then_inc(mT_in[s][b].sem, 16)

            def store(n):
                images = [out[bass.ds(sp.snap(2 * n + b), 1)].rearrange("o t d -> (o t) d") for b in range(2)]
                sp.wait_ge(added[1].sem, added[1].at(n, 4))
                for b, dst in enumerate(images):
                    sp.dma_start(dst[0:1], outb[HALF:HALF + 1, 2 * b, :]).then_inc(out_stored.sem, 16)
                    for a in range(2):
                        sp.dma_start(dst[1 + HALF * a:1 + HALF * (a + 1)],
                                     outb[0:HALF, 2 * b + a, :]).then_inc(out_stored.sem, 16)

            def body(i, store_i, att, load, emb):
                if store_i is not None:
                    store(store_i)
                if att is not None:
                    max_rows(0, att, 0)
                    max_rows(0, att, 1)
                stack_parts(1, i)
                if load is not None:
                    sp.wait_ge(patch_mm.sem, patch_mm.at(emb, 4))
                    load_x(load)
                max_rows(1, i, 0)
                max_rows(1, i, 1)
                if emb is not None:
                    stack_parts(0, emb)

            for dst, src in LOADS:
                sp.dma_start(dst, src).then_inc(weights_in.sem, 16)
            sp.wait_ge(init_done.sem, N_INIT)
            sp.dma_start(gT[FC:FC + 2, 1, :], marks).then_inc(weights_in.sem, 16)
            load_x(0)
            for n in range(2):
                sp.wait_ge(patch_mm.sem, patch_mm.at(n, 4))
                load_x(n + 1)
                stack_parts(0, n)
                if n == 0:
                    max_rows(0, 0, 0)
                    max_rows(0, 0, 1)
            body(0, None, 1, 3, 2)
            with sp.Fori(1, PAIRS - 3) as i:
                body(i, sp.snap(i - 1), sp.snap(i + 1), sp.snap(i + 3), sp.snap(i + 2))
            body(PAIRS - 3, PAIRS - 4, PAIRS - 2, None, PAIRS - 1)
            body(PAIRS - 2, PAIRS - 3, PAIRS - 1, None, None)
            body(PAIRS - 1, PAIRS - 2, None, None, None)
            store(PAIRS - 1)
            sp.wait_ge(out_stored.sem, out_stored.at(PAIRS - 1, out_stored.per))

        N_WEIGHTS = 16 * (len(LOADS) + 1)

        @block.gpsimd
        def _(pool):
            fills = [(xb[:, :, :, :], 1.0), (gT[:, :, :], 0.0), (V[0][:, :, :, :], 0.0), (V[1][:, :, :, :], 0.0),
                     (mx[:, :, :, :], 0.0), (comb[:, :, :], 1.0), (lg[:, :, :], 0.0), (ve[0][:, :, :], 1.0),
                     (ve[1][:, :, :], 1.0), (ve[2][:, :, :], 1.0), (half_s[:, :, :], -0.5),
                     (Ks[0][SR:SR + PARTS, :, :], 1.0), (Ks[1][SR:SR + PARTS, :, :], 1.0), (nT2[:, :, :], 1.0), (P[:, :, :], 0.0), (h1[:, :, :], 0.0),
                     (V[0][:, :, :, HD:HD + 1], 1.0), (V[1][:, :, :, HD:HD + 1], 1.0)]
            assert len(fills) == N_INIT
            for k, (dst, value) in enumerate(fills):
                pool.memset(dst, value).then_inc(init_done.sem, 1)
                pool.wait_ge(init_done.sem, k + 1)

            def rsqrt(which, n, tiles, used):
                t = tiles[0]
                if later(n):
                    pool.wait_ge(used.sem, used.at(n - 1, 4))
                pool.wait_ge(var_done[which].sem, var_done[which].at(n, t + 2))
                pool.tensor_tensor(rstd[which][:, t:t + 2, :], ve[which][:, t:t + 2, :], half_s[:, 0:2, :],
                                   ALU.pow).then_inc(rstd_done[which].sem, 1)

            def cut(s, n):
                for m in range(4):
                    pool.wait_ge(rest_done[s].sem, rest_done[s].at(n, m + 1))
                    hold_wait(pool)
                    pool.tensor_copy(parts[s][:, m, 1, :], rest[:, m, :]).then_inc(mid_done[s].sem, 1)
                    pool.wait_ge(mid_done[s].sem, mid_done[s].at(n, m + 1))
                    pool.tensor_tensor(parts[s][:, m, 2, :], rest[:, m, :], parts[s][:, m, 1, :],
                                       ALU.subtract).then_inc(lo_done[s].sem, 1)

            def keep(n):
                pool.wait_ge(h1_copied.sem, h1_copied.at(n, 4))
                if later(n):
                    pool.wait_ge(added[0].sem, added[0].at(n - 1, 4))
                hold_wait(pool)
                pool.tensor_copy(h1k[:, :, :], h1[:, :, :]).then_inc(kept.sem, 1)

            def embed(n):
                rsqrt(0, n, (0, 1), h0_normed)
                rsqrt(0, n, (2, 3), h0_normed)
                rsqrt(1, n, (0, 1), n1_normed)
                rsqrt(1, n, (2, 3), n1_normed)
                cut(0, n)

            def body(i, att, emb):
                rsqrt(2, i, (0, 1), n2_normed)
                rsqrt(2, i, (2, 3), n2_normed)
                if att is not None:
                    keep(att)
                cut(1, i)
                if emb is not None:
                    embed(emb)

            embed(0)
            keep(0)
            embed(1)
            body(0, 1, 2)
            with pool.Fori(1, PAIRS - 2) as i:
                body(i, i + 1, i + 2)
            body(PAIRS - 2, PAIRS - 1, None)
            body(PAIRS - 1, None, None)

        @block.tensor
        def _(pe):

            def patch(n, t, before):
                b, a = divmod(t, 2)
                if t == 0:
                    pe.wait_ge(x_in.sem, x_in.at(n, x_in.per))
                if t >= 2:
                    pe.wait_ge(h0_normed.sem, h0_normed.at(n, t - 1))
                elif before is not None:
                    pe.wait_ge(before[0].sem, before[0].at(before[1], t + 3))
                for q in range(QH):
                    k = 2 * XR + (q == 0)
                    mm = pe.matmul(ps[0:HALF, 6 + a, 0:D],
                                   xb[0:k, b, 7 * a:7 * a + 7, q:q + PATCH * (GRID - 1) + 1:PATCH],
                                   w1_s[0:k, q, :], start=(q == 0), stop=(q == QH - 1))
                mm.then_inc(patch_mm.sem, 1)

            def turn_h0(n, a):
                pe.wait_ge(h0_normed.sem, h0_normed.at(n, 3 + a))
                for b in range(2):
                    for c in range(2):
                        mm = pe.transpose(ps[0:FC, 6 + a, (2 * c + b) * HALF:(2 * c + b + 1) * HALF],
                                          h0n[:, 2 * b + a, c * FC:(c + 1) * FC], id_s[0:HALF, 0:HALF])
                mm.then_inc(h0T_mm.sem, 1)

            def second(n, t):
                a = t % 2
                pe.wait_ge(gelu_done.sem, gelu_done.at(n, 4))
                if t >= 2:
                    pe.wait_ge(h1_copied.sem, h1_copied.at(n, t - 1))
                dst = ps[0:ROWS[a], 6 + a, 0:D]
                pe.matmul(dst, gT[0:FC, 0, tile_cols(t)], w2_s[0:FC, 0, :], start=True, stop=False)
                pe.matmul(dst, gT[0:FC + 2, 1, tile_cols(t)], w2_s[0:FC + 2, 1, :],
                          start=False, stop=True).then_inc(w2_mm.sem, 1)

            def turn_n1(n, t):
                a = t % 2
                pe.wait_ge(n1_normed.sem, n1_normed.at(n, t + 1))
                if t < 2:
                    pe.wait_ge(h1_copied.sem, h1_copied.at(n, t + 3))
                else:
                    pe.wait_ge(n1T_copied.sem, n1T_copied.at(n, t - 1))
                for c in range(2):
                    mm = pe.transpose(ps[0:FC, 6 + a, c * 128:c * 128 + ROWS[a]],
                                      n1[0:ROWS[a], t, c * FC:(c + 1) * FC], id_s[0:ROWS[a], 0:ROWS[a]])
                mm.then_inc(n1T_mm.sem, 1)

            def qk1(n, m):
                if m == 0:
                    pe.wait_ge(n1T_copied.sem, n1T_copied.at(n, 4))
                if m >= 2:
                    pe.wait_ge(rest_done[0].sem, rest_done[0].at(n, m - 1))
                for c in range(2):
                    mm = pe.matmul(ps[0:FC, 6 + m % 2, 0:PT], wqkv_s[0][:, c, m * FC:(m + 1) * FC], nT1[:, c, :],
                                   start=(c == 0), stop=(c == 1))
                mm.then_inc(qk_mm[0].sem, 1)

            def v1(n, t):
                a = t % 2
                if t < 2:
                    pe.wait_ge(rest_done[0].sem, rest_done[0].at(n, t + 3))
                else:
                    pe.wait_ge(v_copied[0].sem, v_copied[0].at(n, t - 1))
                for c in range(2):
                    mm = pe.matmul(ps[0:ROWS[a], 6 + a, 0:D], nT1[:, c, tile_cols(t)], wqkv_s[0][:, c, 2 * D:3 * D],
                                   start=(c == 0), stop=(c == 1))
                mm.then_inc(v_mm[0].sem, 1)

            def project(s, n, t, before):
                r = ROWS[t % 2]
                if t >= 2:
                    pe.wait_ge(added[s].sem, added[s].at(n, t - 1))
                else:
                    pe.wait_ge(before[0].sem, before[0].at(before[1], t + 3))
                pe.wait_ge(divided[s].sem, divided[s].at(n, GROUPS))
                for g in range(GROUPS):
                    mm = pe.matmul(ps[0:r, 6 + t % 2, 0:D], O[s][:, g, tile_cols(t)], wo_s[s][:, g, :],
                                   start=(g == 0), stop=(g == GROUPS - 1))
                mm.then_inc(wo_mm[s].sem, 1)

            def turn_n2(n, t):
                r = ROWS[t % 2]
                pe.wait_ge(n2_normed.sem, n2_normed.at(n, t + 1))
                if t < 2:
                    pe.wait_ge(added[0].sem, added[0].at(n, t + 3))
                else:
                    pe.wait_ge(n2T_copied.sem, n2T_copied.at(n, t - 1))
                for c in range(2):
                    mm = pe.transpose(ps[0:FC, 6 + t % 2, c * 128:c * 128 + r],
                                      n2[0:r, t, c * FC:(c + 1) * FC], id_s[0:r, 0:r])
                mm.then_inc(n2T_mm.sem, 1)

            def gate(n, t):
                if t < 2:
                    pe.wait_ge(n2T_copied.sem, n2T_copied.at(n, t + 3))
                else:
                    pe.wait_ge(n2T_copied.sem, n2T_copied.at(n, 4))
                c0 = tile_cols(t).start
                dst = ps[0:HALF + 1, 6 + t % 2, 256 * (t // 2):256 * (t // 2) + ER + EXPERTS]
                pe.matmul(dst, nT2[0:FC, 0, c0:c0 + HALF + 1], wgl_s[0:FC, 0, :], start=True, stop=False)
                pe.matmul(dst, nT2[0:FC + 1, 1, c0:c0 + HALF + 1], wgl_s[0:FC + 1, 1, :], start=False,
                          stop=True).then_inc(gate_mm.sem, 1)

            def turn_hw(n, t):
                r = ROWS[t % 2]
                pe.wait_ge(hw_done.sem, hw_done.at(n, 1))
                if t < 2:
                    pe.wait_ge(gate_copied.sem, gate_copied.at(n, t + 1))
                else:
                    pe.wait_ge(hwT_copied.sem, hwT_copied.at(n, t - 1))
                pe.transpose(ps[0:ER, 6 + t % 2, 0:r], hw[0:r, t, :], id_s[0:r, 0:r])
                pe.transpose(ps[0:1 + EXPERTS, 6 + t % 2, 128:128 + r], comb[0:r, t, :],
                             id_s[0:r, 0:r]).then_inc(hwT_mm.sem, 1)

            def qk2(n, m):
                if m == 0:
                    pe.wait_ge(hwT_copied.sem, hwT_copied.at(n, 4))
                if m >= 2:
                    pe.wait_ge(rest_done[1].sem, rest_done[1].at(n, m - 1))
                dst = ps[0:FC, 6 + m % 2, 0:PT]
                cols = slice(m * FC, (m + 1) * FC)
                pe.matmul(dst, wqkv_s[1][0:FC, 0, cols], nT2[0:FC, 0, 0:PT], start=True, stop=False)
                pe.matmul(dst, wqkv_s[1][:, 1, cols], nT2[:, 1, 0:PT], start=False, stop=False)
                pe.matmul(dst, wlora_s[:, cols], hwT[:, :], start=False, stop=True).then_inc(qk_mm[1].sem, 1)

            def v2(n, t):
                r = ROWS[t % 2]
                if t < 2:
                    pe.wait_ge(rest_done[1].sem, rest_done[1].at(n, t + 3))
                else:
                    pe.wait_ge(v_copied[1].sem, v_copied[1].at(n, t - 1))
                dst = ps[0:r, 6 + t % 2, 0:D]
                cols = slice(2 * D, 3 * D)
                pe.matmul(dst, nT2[0:FC, 0, tile_cols(t)], wqkv_s[1][0:FC, 0, cols], start=True, stop=False)
                pe.matmul(dst, nT2[:, 1, tile_cols(t)], wqkv_s[1][:, 1, cols], start=False, stop=False)
                pe.matmul(dst, hwT[:, tile_cols(t)], wlora_s[:, cols], start=False, stop=True).then_inc(v_mm[1].sem, 1)

            def pass1(s, n, u, before):
                b, a, g = u // 6, u // 3 % 2, u % 3
                if u == 0:
                    pe.wait_ge(stacks_in[s].sem, stacks_in[s].at(n, stacks_in[s].per))
                if u >= 2:
                    pe.wait_ge(max_done[s].sem, max_done[s].at(n, u - 1))
                elif before is not None:
                    pe.wait_ge(exp_done[before[0]].sem, exp_done[before[0]].at(before[1], 11 + u))
                z, r = u % 2, ROWS[a]
                keys = ROWS[0] if (s == 0 and a == 0) else TOK
                for h in range(GH):
                    hd = GH * g + h
                    dst = ps[0:r, 2 * z + h // 2, (h % 2) * TOK:(h % 2) * TOK + keys]
                    mm = pe.matmul(dst, Qs[s][0:SR, hd, tile_cols(2 * b + a)],
                                   Ks[s][0:SR, hd, b * TOK:b * TOK + keys], start=True, stop=(s == 1))
                    if s == 0:
                        c0 = (h % 2) * TOK + a * ROWS[0]
                        mm = pe.matmul(ps[0:r, 2 * z + h // 2, c0:c0 + r], idb_s[0:r, 0:r],
                                       mask_s[0:r, a, 0:r], start=False, stop=True)
                mm.then_inc(p1_mm[s].sem, 1)

            def turn_max(s, n, b, before):
                pe.wait_ge(max_parts[s].sem, max_parts[s].at(n, b + 1))
                if before is not None:
                    pe.wait_ge(divided[before[0]].sem, divided[before[0]].at(before[1], GROUPS))
                for a in range(2):
                    mm = pe.matmul(ps[0:PARTS * HEADS, 4 + b, a * ROWS[0]:a * ROWS[0] + ROWS[a]],
                                   mxp[0:ROWS[a], b, a, :, :].rearrange("p r h -> p (r h)"), idb_s[0:ROWS[a], 0:ROWS[a]],
                                   start=True, stop=True)
                mm.then_inc(mT_mm[s].sem, 1)

            def pass2(s, n, v):
                b, g = divmod(v, GROUPS)
                if g == 0:
                    pe.wait_ge(mT_in[s][b].sem, mT_in[s][b].at(n, 16))
                for a in range(2):
                    u = 2 * v + a
                    if u >= 2:
                        pe.wait_ge(exp_done[s].sem, exp_done[s].at(n, u - 1))
                    else:
                        pe.wait_ge(max_done[s].sem, max_done[s].at(n, 11 + u))
                    z, r = u % 2, ROWS[a]
                    lo = ROWS[0] if (s == 0 and a == 1) else 0
                    for h in range(GH):
                        hd = GH * g + h
                        c0 = (h % 2) * TOK
                        mm = pe.matmul(ps[0:r, 2 * z + h // 2, c0 + lo:c0 + TOK],
                                       Ks[s][0:SR + PARTS, hd, tile_cols(2 * b + a)],
                                       Qs[s][0:SR + PARTS, hd, b * TOK + lo:(b + 1) * TOK], start=True, stop=(s == 1))
                        if s == 0:
                            c0 += a * ROWS[0]
                            mm = pe.matmul(ps[0:r, 2 * z + h // 2, c0:c0 + r], idb_s[0:r, 0:r],
                                           mask_s[0:r, 2 + a, 0:r], start=False, stop=True)
                    mm.then_inc(p2_mm[s].sem, 1)

            def av(s, n, v):
                b, g = divmod(v, GROUPS)
                if v == 0:
                    pe.wait_ge(v_copied[s].sem, v_copied[s].at(n, 4))
                pe.wait_ge(exp_done[s].sem, exp_done[s].at(n, 2 * v + 2))
                if v < 2:
                    pe.wait_ge(mT_copied[s].sem, mT_copied[s].at(n, v + 1))
                else:
                    pe.wait_ge(av_copied[s].sem, av_copied[s].at(n, v - 1 if v < 4 else v))
                bank = 4 + v % 2 if v < 4 else 5
                for a in range(2):
                    lo = ROWS[0] if (s == 0 and a == 1) else 0
                    for h in range(GH):
                        mm = pe.matmul(ps[32 * h:32 * h + 32, bank, lo:TOK],
                                       V[s][:, 2 * b + a, GH * g + h, :],
                                       P[:, (2 * v + a) % 4, h * TOK + lo:(h + 1) * TOK],
                                       start=(a == 0), stop=(a == 1))
                mm.then_inc(av_mm[s].sem, 1)

            def sums(s, n, g):
                pe.wait_ge(av_copied[s].sem, av_copied[s].at(n, 4 + g))
                if g >= 1:
                    pe.wait_ge(divided[s].sem, divided[s].at(n, g))
                pe.matmul(ps[:, 4, 0:PT], sel_s[:, :], O[s][:, g, :], start=True, stop=True).then_inc(sum_mm[s].sem, 1)

            def embed(n, before):
                for t in range(4):
                    patch(n, t, before)
                for a in range(2):
                    turn_h0(n, a)
                for t in range(4):
                    second(n, t)
                for t in range(4):
                    turn_n1(n, t)
                for m in range(4):
                    qk1(n, m)
                for t in range(4):
                    v1(n, t)

            def first_attention(n):
                for u in range(12):
                    pass1(0, n, u, None)
                for b in range(2):
                    turn_max(0, n, b, None)
                for v in range(6):
                    pass2(0, n, v)
                    if v >= 1:
                        av(0, n, v - 1)
                sums(0, n, 0)
                sums(0, n, 1)
                av(0, n, 5)
                sums(0, n, 2)

            def body(i, done, att, emb, p1_before, p0_before):
                def side(stage, *args):
                    if done is not None or stage is not project or args[0] == 0:
                        stage(*args)

                def a0(stage, *args):
                    if att is not None:
                        stage(0, att, *args)

                def d1(stage, *args):
                    if emb is not None:
                        stage(emb, *args)

                e0 = (1, i - 1) if done is not None else None
                e1 = (0, att) if att is not None else (1, i - 1)
                side(project, 1, done, 0, p1_before)
                side(project, 1, done, 1, p1_before)
                a0(pass1, 0, e0)
                a0(pass1, 1, e0)
                side(project, 1, done, 2, p1_before)
                a0(pass1, 2, e0)
                side(project, 1, done, 3, p1_before)
                a0(pass1, 3, e0)
                project(0, i, 0, p0_before)
                a0(pass1, 4, e0)
                project(0, i, 1, p0_before)
                a0(pass1, 5, e0)
                project(0, i, 2, p0_before)
                a0(pass1, 6, e0)
                project(0, i, 3, p0_before)
                a0(pass1, 7, e0)
                a0(turn_max, 0, e0)
                a0(pass1, 8, e0)
                a0(pass1, 9, e0)
                turn_n2(i, 0)
                turn_n2(i, 1)
                a0(pass1, 10, e0)
                a0(pass1, 11, e0)
                turn_n2(i, 2)
                turn_n2(i, 3)
                a0(pass2, 0)
                gate(i, 0)
                gate(i, 1)
                a0(turn_max, 1, e0)
                a0(pass2, 1)
                gate(i, 2)
                gate(i, 3)
                a0(av, 0)
                a0(pass2, 2)
                a0(av, 1)
                a0(pass2, 3)
                a0(av, 2)
                a0(pass2, 4)
                for t in range(4):
                    turn_hw(i, t)
                a0(av, 3)
                qk2(i, 0)
                a0(pass2, 5)
                a0(sums, 0)
                qk2(i, 1)
                a0(av, 4)
                qk2(i, 2)
                a0(sums, 1)
                a0(av, 5)
                qk2(i, 3)
                a0(sums, 2)
                for t in range(4):
                    v2(i, t)
                for t in range(3):
                    d1(patch, t, (v_copied[1], i))
                pass1(1, i, 0, e1)
                pass1(1, i, 1, e1)
                d1(patch, 3, (v_copied[1], i))
                pass1(1, i, 2, e1)
                pass1(1, i, 3, e1)
                pass1(1, i, 4, e1)
                pass1(1, i, 5, e1)
                d1(turn_h0, 0)
                d1(turn_h0, 1)
                pass1(1, i, 6, e1)
                pass1(1, i, 7, e1)
                d1(second, 0)
                turn_max(1, i, 0, e1)
                pass1(1, i, 8, e1)
                d1(second, 1)
                pass1(1, i, 9, e1)
                d1(second, 2)
                pass1(1, i, 10, e1)
                d1(second, 3)
                pass1(1, i, 11, e1)
                pass2(1, i, 0)
                d1(turn_n1, 0)
                d1(turn_n1, 1)
                turn_max(1, i, 1, e1)
                d1(turn_n1, 2)
                d1(turn_n1, 3)
                pass2(1, i, 1)
                d1(qk1, 0)
                av(1, i, 0)
                pass2(1, i, 2)
                d1(qk1, 1)
                av(1, i, 1)
                d1(qk1, 2)
                pass2(1, i, 3)
                av(1, i, 2)
                d1(qk1, 3)
                pass2(1, i, 4)
                av(1, i, 3)
                d1(v1, 0)
                pass2(1, i, 5)
                sums(1, i, 0)
                d1(v1, 1)
                av(1, i, 4)
                d1(v1, 2)
                sums(1, i, 1)
                av(1, i, 5)
                d1(v1, 3)
                sums(1, i, 2)

            pe.wait_ge(weights_in.sem, N_WEIGHTS)
            pe.wait_ge(init_done.sem, N_INIT)
            embed(0, None)
            first_attention(0)
            embed(1, (v_copied[0], 0))
            body(0, None, 1, 2, None, (v_copied[0], 1))
            with pe.Fori(1, PAIRS - 2) as i:
                body(i, i - 1, i + 1, i + 2, (v_copied[0], i + 1), (added[1], i - 1))
            body(PAIRS - 2, PAIRS - 3, PAIRS - 1, None, (v_copied[0], PAIRS - 1), (added[1], PAIRS - 3))
            body(PAIRS - 1, PAIRS - 2, None, None, (v_copied[1], PAIRS - 2), (added[1], PAIRS - 2))
            for t in range(4):
                project(1, PAIRS - 1, t, (v_copied[1], PAIRS - 1))

        @block.scalar
        def _(act):
            def gelu(n):
                for a in range(2):
                    act.wait_ge(h0T_mm.sem, h0T_mm.at(n, a + 1))
                    if a == 0 and later(n):
                        act.wait_ge(w2_mm.sem, w2_mm.at(n - 1, 4))
                    for c in range(2):
                        lo = a * ROWS[0]
                        dst = gT[0:FC, c, :].rearrange("p (b k) -> p b k", b=2)[:, :, lo:lo + HALF]
                        src = ps[0:FC, 6 + a, 2 * c * HALF:(2 * c + 2) * HALF].rearrange("p (b k) -> p b k", b=2)
                        nc.scalar.activation(dst, src, ACT.Gelu, bias=lnp_s[:, c, 1:2],
                                             scale=lnp_s[:, c, 0:1]).then_inc(gelu_done.sem, 1)

            def copy_h1(n, t):
                act.wait_ge(w2_mm.sem, w2_mm.at(n, t + 1))
                if t == 0 and later(n):
                    act.wait_ge(kept.sem, kept.at(n - 1, 1))
                    act.wait_ge(n1_normed.sem, n1_normed.at(n - 1, 4))
                nc.scalar.activation(h1[0:ROWS[t % 2], t, :], ps[0:ROWS[t % 2], 6 + t % 2, 0:D],
                                     ACT.Copy).then_inc(h1_copied.sem, 1)

            def copy_nT1(n, t):
                act.wait_ge(n1T_mm.sem, n1T_mm.at(n, t + 1))
                if t == 0 and later(n):
                    act.wait_ge(v_mm[0].sem, v_mm[0].at(n - 1, 4))
                src = ps[0:FC, 6 + t % 2, 0:256].rearrange("p (c k) -> p c k", c=2)[:, :, 0:ROWS[t % 2]]
                nc.scalar.activation(nT1[:, :, tile_cols(t)], src, ACT.Copy).then_inc(n1T_copied.sem, 1)

            def high(s, n, m):
                if m == 0 and later(n):
                    act.wait_ge(parts_out[s].sem, parts_out[s].at(n - 1, 4 * 16))
                act.wait_ge(qk_mm[s].sem, qk_mm[s].at(n, m + 1))
                nc.scalar.activation(parts[s][:, m, 0, :], ps[0:FC, 6 + m % 2, 0:PT], ACT.Copy).then_inc(hi_done[s].sem, 1)

            def copy_v(s, n, t):
                act.wait_ge(v_mm[s].sem, v_mm[s].at(n, t + 1))
                if t == 0 and later(n):
                    act.wait_ge(av_mm[s].sem, av_mm[s].at(n - 1, 6))
                nc.scalar.activation(V[s][0:ROWS[t % 2], t, :, 0:HD],
                                     ps[0:ROWS[t % 2], 6 + t % 2, 0:D].rearrange("p (h d) -> p h d", d=HD),
                                     ACT.Copy).then_inc(v_copied[s].sem, 1)

            def copy_mT(s, n, b, before):
                act.wait_ge(mT_mm[s].sem, mT_mm[s].at(n, b + 1))
                if b == 0 and before is not None:
                    act.wait_ge(mT_out[before[0]].sem, mT_out[before[0]].at(before[1], 32))
                nc.scalar.activation(mT[:, b, :], ps[0:PARTS * HEADS, 4 + b, 0:TOK],
                                     ACT.Copy).then_inc(mT_copied[s].sem, 1)

            def copy_av(s, n, v):
                b, g = divmod(v, GROUPS)
                act.wait_ge(av_mm[s].sem, av_mm[s].at(n, v + 1))
                if v == 0 and later(n):
                    act.wait_ge(wo_mm[s].sem, wo_mm[s].at(n - 1, 4))
                nc.scalar.activation(O[s][:, g, b * TOK:(b + 1) * TOK], ps[:, 4 + v % 2 if v < 4 else 5, 0:TOK],
                                     ACT.Copy).then_inc(av_copied[s].sem, 1)

            def exps(s, n, v):
                for a in range(2):
                    u = 2 * v + a
                    act.wait_ge(p2_mm[s].sem, p2_mm[s].at(n, u + 1))
                    if u >= 4:
                        act.wait_ge(av_mm[s].sem, av_mm[s].at(n, v - 1))
                    lo = ROWS[0] if (s == 0 and a == 1) else 0
                    dst = P[0:ROWS[a], u % 4, :].rearrange("p (k h c) -> p k h c", k=2, h=2)[:, :, :, lo:TOK]
                    nc.scalar.activation(dst, score_slot(u % 2, ROWS[a], lo, TOK - lo), ACT.Exp,
                                         scale=SCALE).then_inc(exp_done[s].sem, 1)

            def copy_nT2(n, t):
                act.wait_ge(n2T_mm.sem, n2T_mm.at(n, t + 1))
                if t == 0 and later(n):
                    act.wait_ge(v_mm[1].sem, v_mm[1].at(n - 1, 4))
                src = ps[0:FC, 6 + t % 2, 0:256].rearrange("p (c k) -> p c k", c=2)[:, :, 0:ROWS[t % 2]]
                nc.scalar.activation(nT2[0:FC, :, tile_cols(t)], src, ACT.Copy).then_inc(n2T_copied.sem, 1)

            def copy_gate(n, a):
                act.wait_ge(gate_mm.sem, gate_mm.at(n, 3 + a))
                src = ps[0:HALF + 1, 6 + a, :].rearrange("p (b k) -> p b k", b=2)[:, :, 0:ER + EXPERTS]
                nc.scalar.activation(gs[:, a:4:2, :], src, ACT.Copy).then_inc(gate_copied.sem, 1)

            def gate_exps(n):
                act.wait_ge(logits_done.sem, logits_done.at(n, 1))
                nc.scalar.activation(pe_[:, :, :], lg[:, :, :], ACT.Exp).then_inc(gate_exp.sem, 1)

            def copy_hwT(n, t):
                act.wait_ge(hwT_mm.sem, hwT_mm.at(n, t + 1))
                nc.scalar.activation(hwT[:, tile_cols(t)], ps[0:ER, 6 + t % 2, 0:ROWS[t % 2]], ACT.Copy)
                nc.scalar.activation(nT2[FC:FC + 1 + EXPERTS, 1, tile_cols(t)],
                                     ps[0:1 + EXPERTS, 6 + t % 2, 128:128 + ROWS[t % 2]], ACT.Copy).then_inc(hwT_copied.sem, 1)

            def embed(n):
                gelu(n)
                for t in range(4):
                    copy_h1(n, t)
                for t in range(4):
                    copy_nT1(n, t)
                for m in range(4):
                    high(0, n, m)
                for t in range(4):
                    copy_v(0, n, t)

            def first_attention(n):
                copy_mT(0, n, 0, None)
                copy_mT(0, n, 1, None)
                for v in range(6):
                    exps(0, n, v)
                    if v >= 1:
                        copy_av(0, n, v - 1)
                copy_av(0, n, 5)

            def body(i, done, att, emb):
                def a0(stage, *args):
                    if att is not None:
                        stage(0, att, *args)

                def d1(stage, *args):
                    if emb is not None:
                        stage(*args)

                m0 = (1, i - 1) if done is not None else (0, 0)
                m1 = (0, att) if att is not None else (1, i - 1)
                a0(copy_mT, 0, m0)
                copy_nT2(i, 0)
                copy_nT2(i, 1)
                copy_nT2(i, 2)
                copy_nT2(i, 3)
                a0(exps, 0)
                a0(copy_mT, 1, m0)
                a0(exps, 1)
                copy_gate(i, 0)
                copy_gate(i, 1)
                a0(copy_av, 0)
                a0(exps, 2)
                gate_exps(i)
                a0(copy_av, 1)
                a0(exps, 3)
                a0(copy_av, 2)
                a0(exps, 4)
                for t in range(4):
                    copy_hwT(i, t)
                a0(copy_av, 3)
                high(1, i, 0)
                a0(exps, 5)
                high(1, i, 1)
                a0(copy_av, 4)
                high(1, i, 2)
                a0(copy_av, 5)
                high(1, i, 3)
                for t in range(4):
                    copy_v(1, i, t)
                d1(gelu, emb)
                copy_mT(1, i, 0, m1)
                for t in range(4):
                    d1(copy_h1, emb, t)
                exps(1, i, 0)
                for t in range(2):
                    d1(copy_nT1, emb, t)
                copy_mT(1, i, 1, m1)
                for t in range(2, 4):
                    d1(copy_nT1, emb, t)
                exps(1, i, 1)
                d1(high, 0, emb, 0)
                copy_av(1, i, 0)
                exps(1, i, 2)
                d1(high, 0, emb, 1)
                copy_av(1, i, 1)
                d1(high, 0, emb, 2)
                exps(1, i, 3)
                copy_av(1, i, 2)
                d1(high, 0, emb, 3)
                exps(1, i, 4)
                copy_av(1, i, 3)
                d1(copy_v, 0, emb, 0)
                exps(1, i, 5)
                d1(copy_v, 0, emb, 1)
                copy_av(1, i, 4)
                d1(copy_v, 0, emb, 2)
                copy_av(1, i, 5)
                d1(copy_v, 0, emb, 3)

            act.wait_ge(weights_in.sem, N_WEIGHTS)
            act.wait_ge(init_done.sem, N_INIT)
            embed(0)
            first_attention(0)
            embed(1)
            body(0, None, 1, 2)
            with act.Fori(1, PAIRS - 2) as i:
                body(i, i - 1, i + 1, i + 2)
            body(PAIRS - 2, PAIRS - 3, PAIRS - 1, None)
            body(PAIRS - 1, PAIRS - 2, None, None)

        @block.vector
        def _(dve):
            at = {}

            def reset():
                for chain in (dve_here, *dve_stats, *dve_max, *dve_div):
                    at[chain] = 0

            def link(chain, n, ins):
                ins.then_inc(chain.sem, 1)
                at[chain] += 1
                dve.wait_ge(chain.sem, chain.at(n, at[chain]))

            def moments(which, n, src, r, t):
                link(dve_stats[which], n, dve.bn_stats(st[which][0:r, t, :], src))
                hold_wait(dve)
                link(dve_stats[which], n, dve.bn_aggr(mv[which][0:r, t, :], st[which][0:r, t, :]))
                dve.tensor_scalar(ve[which][0:r, t, :], mv[which][0:r, t, 1:2], EPS, None,
                                  ALU.add).then_inc(var_done[which].sem, 1)

            def scale(which, n, dst, src, r, t, done):
                dve.wait_ge(rstd_done[which].sem, rstd_done[which].at(n, t // 2 + 1))
                dve.tensor_scalar(dst, src, mv[which][0:r, t, 0:1], rstd[which][0:r, t, :],
                                  ALU.subtract, ALU.mult).then_inc(done.sem, 1)

            def norm_h0(n, tiles):
                for t in tiles:
                    dve.wait_ge(patch_mm.sem, patch_mm.at(n, t + 1))
                    moments(0, n, ps[0:HALF, 6 + t % 2, 0:D], HALF, t)
                for t in tiles:
                    if t == 0 and later(n):
                        dve.wait_ge(h0T_mm.sem, h0T_mm.at(n - 1, 2))
                    scale(0, n, h0n[:, t, :], ps[0:HALF, 6 + t % 2, 0:D], HALF, t, h0_normed)

            def norm_n1(n, tiles):
                for t in tiles:
                    dve.wait_ge(h1_copied.sem, h1_copied.at(n, t + 1))
                    moments(1, n, h1[0:ROWS[t % 2], t, :], ROWS[t % 2], t)
                for t in tiles:
                    if t == 0 and later(n):
                        dve.wait_ge(n1T_mm.sem, n1T_mm.at(n - 1, 4))
                    r = ROWS[t % 2]
                    scale(1, n, n1[0:r, t, :], h1[0:r, t, :], r, t, n1_normed)

            def norm_n2(n, tiles):
                for t in tiles:
                    dve.wait_ge(added[0].sem, added[0].at(n, t + 1))
                    moments(2, n, h2[0:ROWS[t % 2], t, :], ROWS[t % 2], t)
                for t in tiles:
                    if t == 0 and later(n):
                        dve.wait_ge(n2T_mm.sem, n2T_mm.at(n - 1, 4))
                    r = ROWS[t % 2]
                    scale(2, n, n2[0:r, t, :], h2[0:r, t, :], r, t, n2_normed)

            def remainder(s, n, m, before):
                dve.wait_ge(hi_done[s].sem, hi_done[s].at(n, m + 1))
                if before is not None:
                    dve.wait_ge(lo_done[before[0]].sem, lo_done[before[0]].at(before[1], m + 1))
                dve.tensor_tensor(rest[:, m, :], ps[0:FC, 6 + m % 2, 0:PT], parts[s][:, m, 0, :],
                                  ALU.subtract).then_inc(rest_done[s].sem, 1)

            def maximum(s, n, u):
                b, a, g = u // 6, u // 3 % 2, u % 3
                keys = ROWS[0] if (s == 0 and a == 0) else TOK
                dve.wait_ge(p1_mm[s].sem, p1_mm[s].at(n, u + 1))
                dve.tensor_reduce(mx[0:ROWS[a], b, a, GH * g:GH * (g + 1)].rearrange("p (k h) -> p k h", k=2),
                                  score_slot(u % 2, ROWS[a], 0, keys), AX_X, ALU.max).then_inc(max_done[s].sem, 1)

            def max_cut(s, n, b, before):
                dve.wait_ge(max_done[s].sem, max_done[s].at(n, 6 * b + 6))
                if before is not None:
                    dve.wait_ge(mT_mm[before[0]].sem, mT_mm[before[0]].at(before[1], 2))
                m, p = mx[:, b], mxp[:, b]
                link(dve_max[s], n, dve.tensor_scalar(p[:, :, 0, :], m, -1.0, None, ALU.mult))
                link(dve_max[s], n, dve.scalar_tensor_tensor(out=mxr[:, :, :], in0=m, scalar=-1.0, in1=p[:, :, 0, :],
                                                             op0=ALU.mult, op1=ALU.subtract))
                link(dve_max[s], n, dve.tensor_copy(p[:, :, 1, :], mxr[:, :, :]))
                dve.tensor_tensor(p[:, :, 2, :], mxr[:, :, :], p[:, :, 1, :], ALU.subtract).then_inc(max_parts[s].sem, 1)

            def divide(s, n, g):
                dve.wait_ge(sum_mm[s].sem, sum_mm[s].at(n, g + 1))
                link(dve_div[s], n, dve.reciprocal(inv[:, :], ps[:, 4, 0:PT]))
                dve.tensor_tensor(O[s][:, g, :], O[s][:, g, :], inv[:, :], ALU.mult).then_inc(divided[s].sem, 1)
                dve.wait_ge(divided[s].sem, divided[s].at(n, g + 1))

            def add(s, n, t):
                res, dst = (h1k, h2) if s == 0 else (h2, outb)
                r = ROWS[t % 2]
                if s == 0 and t == 0:
                    dve.wait_ge(kept.sem, kept.at(n, 1))
                if s == 1 and t == 0 and later(n):
                    dve.wait_ge(out_stored.sem, out_stored.at(n - 1, out_stored.per))
                dve.wait_ge(wo_mm[s].sem, wo_mm[s].at(n, t + 1))
                dve.tensor_tensor(dst[0:r, t, :], ps[0:r, 6 + t % 2, 0:D], res[0:r, t, :], ALU.add).then_inc(added[s].sem, 1)

            def choose(n):
                def bc(ap):
                    return ap.to_broadcast([HALF + 1, 4, EXPERTS])

                rk = rank_s[:, :].unsqueeze(1).to_broadcast([HALF + 1, 4, EXPERTS])
                logits = gs[:, :, ER:ER + EXPERTS]
                dve.wait_ge(gate_copied.sem, gate_copied.at(n, 2))
                link(dve_here, n, dve.tensor_reduce(gm[:, :, 0], logits, AX_X, ALU.max))
                dve.tensor_tensor(lg[:, :, :], logits, bc(gm[:, :, :]), ALU.subtract).then_inc(logits_done.sem, 1)
                dve.wait_ge(logits_done.sem, logits_done.at(n, 1))
                link(dve_here, n, dve.scalar_tensor_tensor(out=gc[:, :, :], in0=lg[:, :, :], scalar=0.0, in1=rk,
                                                           op0=ALU.is_equal, op1=ALU.mult))
                link(dve_here, n, dve.tensor_reduce(gm[:, :, 0], gc[:, :, :], AX_X, ALU.max))
                link(dve_here, n, dve.tensor_tensor(s1[:, :, :], gc[:, :, :], bc(gm[:, :, :]), ALU.is_equal))
                link(dve_here, n, dve.scalar_tensor_tensor(out=pr[:, :, :], in0=s1[:, :, :], scalar=-BIG,
                                                           in1=lg[:, :, :], op0=ALU.mult, op1=ALU.add))
                link(dve_here, n, dve.tensor_reduce(gm[:, :, 0], pr[:, :, :], AX_X, ALU.max))
                link(dve_here, n, dve.tensor_tensor(ge[:, :, :], pr[:, :, :], bc(gm[:, :, :]), ALU.is_equal))
                link(dve_here, n, dve.tensor_tensor(gc[:, :, :], ge[:, :, :], rk, ALU.mult))
                dve.wait_ge(gate_exp.sem, gate_exp.at(n, 1))
                dve.tensor_reduce(gsum[:, :, 0], pe_[:, :, :], AX_X, ALU.add)
                link(dve_here, n, dve.tensor_reduce(gm[:, :, 0], gc[:, :, :], AX_X, ALU.max))
                dve.reciprocal(gsum[:, :, :], gsum[:, :, :])
                link(dve_here, n, dve.tensor_tensor(s2[:, :, :], gc[:, :, :], bc(gm[:, :, :]), ALU.is_equal))
                link(dve_here, n, dve.tensor_tensor(ge[:, :, :], s1[:, :, :], s2[:, :, :], ALU.add))
                link(dve_here, n, dve.scalar_tensor_tensor(out=pr[:, :, :], in0=pe_[:, :, :], scalar=LORA_SCALE,
                                                           in1=ge[:, :, :], op0=ALU.mult, op1=ALU.mult))
                dve.tensor_tensor(comb[:, :, 1:1 + EXPERTS], pr[:, :, :], bc(gsum[:, :, :]),
                                  ALU.mult).then_inc(comb_done.sem, 1)
                dve.wait_ge(comb_done.sem, comb_done.at(n, 1))
                dve.tensor_tensor(hw[:, :, :].rearrange("p t (e k) -> p t e k", e=EXPERTS),
                                  gs[:, :, 0:ER].rearrange("p t (e k) -> p t e k", e=EXPERTS),
                                  comb[:, :, 1:1 + EXPERTS].unsqueeze(3).to_broadcast([HALF + 1, 4, EXPERTS, RANK]),
                                  ALU.mult).then_inc(hw_done.sem, 1)

            def embed(n, before):
                norm_h0(n, (0, 1))
                norm_h0(n, (2, 3))
                norm_n1(n, (0, 1))
                norm_n1(n, (2, 3))
                for m in range(4):
                    remainder(0, n, m, before)

            def body(i, done, att, emb):
                def a0(stage, *args):
                    if att is not None:
                        stage(0, att, *args)

                def d1(stage, *args):
                    if emb is not None:
                        stage(*args)

                m0 = (1, i - 1) if done is not None else (0, 0)
                m1 = (0, att) if att is not None else (1, i - 1)
                reset()
                if done is not None:
                    add(1, done, 0)
                    add(1, done, 1)
                a0(maximum, 0)
                a0(maximum, 1)
                if done is not None:
                    add(1, done, 2)
                a0(maximum, 2)
                if done is not None:
                    add(1, done, 3)
                a0(maximum, 3)
                add(0, i, 0)
                a0(maximum, 4)
                add(0, i, 1)
                a0(maximum, 5)
                a0(max_cut, 0, m0)
                add(0, i, 2)
                a0(maximum, 6)
                add(0, i, 3)
                norm_n2(i, (0, 1))
                a0(maximum, 7)
                a0(maximum, 8)
                norm_n2(i, (2, 3))
                a0(maximum, 9)
                a0(maximum, 10)
                a0(maximum, 11)
                a0(max_cut, 1, m0)
                choose(i)
                remainder(1, i, 0, (0, att) if att is not None else (1, i - 1))
                a0(divide, 0)
                remainder(1, i, 1, (0, att) if att is not None else (1, i - 1))
                remainder(1, i, 2, (0, att) if att is not None else (1, i - 1))
                a0(divide, 1)
                remainder(1, i, 3, (0, att) if att is not None else (1, i - 1))
                a0(divide, 2)
                d1(norm_h0, emb, (0, 1))
                maximum(1, i, 0)
                maximum(1, i, 1)
                d1(norm_h0, emb, (2, 3))
                for u in range(2, 6):
                    maximum(1, i, u)
                max_cut(1, i, 0, m1)
                for u in range(6, 9):
                    maximum(1, i, u)
                d1(norm_n1, emb, (0, 1))
                for u in range(9, 12):
                    maximum(1, i, u)
                max_cut(1, i, 1, m1)
                d1(norm_n1, emb, (2, 3))
                for m in range(4):
                    d1(remainder, 0, emb, m, (1, i))
                divide(1, i, 0)
                divide(1, i, 1)
                divide(1, i, 2)
                for chain in (dve_here, dve_max[1], dve_div[1]):
                    assert at[chain] == chain.per, (chain.per, at[chain])

            dve.wait_ge(weights_in.sem, N_WEIGHTS)
            dve.wait_ge(init_done.sem, N_INIT)
            reset()
            embed(0, None)
            for u in range(12):
                maximum(0, 0, u)
                if u % 6 == 5:
                    max_cut(0, 0, u // 6, None)
            for g in range(GROUPS):
                divide(0, 0, g)
            reset()
            embed(1, (0, 0))
            body(0, None, 1, 2)
            with dve.Fori(1, PAIRS - 2) as i:
                body(i, i - 1, i + 1, i + 2)
            body(PAIRS - 2, PAIRS - 3, PAIRS - 1, None)
            body(PAIRS - 1, PAIRS - 2, None, None)
            for t in range(4):
                add(1, PAIRS - 1, t)


def kernel(x, cls_tok, L0_tok_W1, L0_tok_b1, L0_tok_ln_w, L0_tok_ln_b, L0_tok_W2, L0_tok_b2,
           L0_attn_wq, L0_attn_wk, L0_attn_wv, L0_attn_wo, L0_ffn_Wg, L0_ffn_bg, L0_ffn_Wqkv, L0_ffn_bqkv,
           L0_ffn_Wproj, L0_ffn_bproj, L0_ffn_A, L0_ffn_ba, L0_ffn_Bm, L0_ffn_bb):
    import numpy as np
    import concourse.bacc as bacc
    from concourse.bass_utils import run_bass_kernel_spmd

    f = np.float32

    def zeros(*shape):
        return np.zeros(shape, f)

    order = np.array([(6 * m + h) * HD + j for m in range(2) for j in range(HD) for h in range(6)])

    def qkv_cols(wt):
        return np.concatenate([wt[:, 0:D][:, order], wt[:, D:2 * D][:, order], wt[:, 2 * D:]], axis=1)

    w1 = zeros(2 * XR + 1, QH, D)
    for s in range(2):
        w1[XR * s:XR * (s + 1)] = L0_tok_W1.reshape(XR, PATCH, D)[:, QH * s:QH * (s + 1)]
    w1[2 * XR, 0] = L0_tok_b1
    w2 = zeros(FC + 2, 2, D)
    w2[0:FC, 0], w2[0:FC, 1] = L0_tok_W2[0:FC], L0_tok_W2[FC:D]
    w2[FC, 1], w2[FC + 1, 1] = L0_tok_b2, cls_tok[0, 0]
    lnp = np.stack([L0_tok_ln_w.reshape(2, FC).T, L0_tok_ln_b.reshape(2, FC).T], axis=2)
    wq1 = qkv_cols(np.concatenate([L0_attn_wq.T, L0_attn_wk.T, L0_attn_wv.T], axis=1))
    wqkv1 = wq1.reshape(2, FC, 3 * D).transpose(1, 0, 2)
    wq2 = qkv_cols(L0_ffn_Wqkv.T)
    wqkv2 = zeros(FC + 1 + EXPERTS, 2, 3 * D)
    wqkv2[0:FC] = wq2.reshape(2, FC, 3 * D).transpose(1, 0, 2)
    wqkv2[FC, 1] = qkv_cols(L0_ffn_bqkv[None])[0]
    wqkv2[FC + 1:, 1] = qkv_cols(L0_ffn_bb)
    wlora = qkv_cols(L0_ffn_Bm.transpose(0, 2, 1).reshape(ER, 3 * D))
    wgl = zeros(FC + 1, 2, ER + EXPERTS)
    wgl[0:FC, :, 0:ER] = L0_ffn_A.reshape(ER, D).T.reshape(2, FC, ER).transpose(1, 0, 2)
    wgl[0:FC, :, ER:] = L0_ffn_Wg.T.reshape(2, FC, EXPERTS).transpose(1, 0, 2)
    wgl[FC, 1, 0:ER], wgl[FC, 1, ER:] = L0_ffn_ba.reshape(ER), L0_ffn_bg

    def wo_rows(wt):
        r = zeros(GH, 32, GROUPS, D)
        r[:, 0:HD] = wt.reshape(GROUPS, GH, HD, D).transpose(1, 2, 0, 3)
        return r.reshape(128, GROUPS, D)

    wo1, wo2 = wo_rows(L0_attn_wo.T), wo_rows(L0_ffn_Wproj.T)
    wo2[HD, 0] = L0_ffn_bproj

    ident = np.eye(128, dtype=f)
    bf = mybir.dt.np(BF16) if hasattr(mybir.dt, "np") else __import__("ml_dtypes").bfloat16
    seq = [np.array(list(range(1, HALF + 1)) + [0]), np.arange(HALF)]
    masks = np.zeros((HALF + 1, 4, HALF + 1), f)
    for a in range(2):
        r = ROWS[a]
        late = np.where(seq[a][None, :] > seq[a][:, None], f(-1e9), f(0))
        masks[0:r, a, 0:r] = late
        masks[0:r, 2 + a, 0:r] = late.T
    sel = zeros(128, 128)
    for h in range(GH):
        sel[32 * h + HD, 32 * h:32 * h + 32] = 1
    marks = np.ones((2, PT), f)
    for b in range(2):
        marks[0, b * TOK + HALF] = 0
    marks[1] = 1 - marks[0]
    rank8 = np.tile(np.arange(EXPERTS, 0, -1, dtype=f), (HALF + 1, 1))

    arrays = dict(x=x, w1=w1, w2=w2, lnp=lnp, wqkv1=wqkv1, wo1=wo1, wgl=wgl, wqkv2=wqkv2, wlora=wlora, wo2=wo2,
                  ident=ident, identb=ident.astype(bf), masks=masks.astype(bf), sel=sel, marks=marks, rank8=rank8)
    nc = bacc.Bacc("TRN2", target_bir_lowering=False, num_devices=1)
    named, args = {}, []
    for name, a in arrays.items():
        a = np.ascontiguousarray(a)
        named[f"in_{name}"] = a
        args.append(nc.dram_tensor(f"in_{name}", a.shape, mybir.dt.from_np(a.dtype), kind="ExternalInput").ap())
    out = nc.dram_tensor("out_0", (IMAGES, TOK, D), F32, kind="ExternalOutput").ap()
    vit_tower(nc, *args, out)
    r = run_bass_kernel_spmd(nc, [named], core_ids=[0])
    return r.results[0]["out_0"]
```

```python
from contextlib import ExitStack

import concourse.bass as bass
from concourse import mybir

F32 = mybir.dt.float32
BF16 = mybir.dt.bfloat16
ALU = mybir.AluOpType
ACT = mybir.ActivationFunctionType
AX_X = mybir.AxisListType.X

IMAGES, CHANNELS, IMG = 128, 3, 224
PATCH = 16
GRID = IMG // PATCH
D = 192
HEADS, HD = 12, 16
TOK = GRID * GRID + 1
HALF = GRID * GRID // 2
ROWS = [HALF + 1, HALF]
PAIRS = IMAGES // 2
TR = HALF + 1
PT = 4 * TR
FC = D // 2
QH = PATCH // 2
XR = CHANNELS * PATCH
EXPERTS, RANK = 8, 16
ER = EXPERTS * RANK
GH = 4
GROUPS = HEADS // GH
PARTS = 3
SR = 6 * HD
EPS = 1e-5
SCALE = float(HD) ** -0.5
LORA_SCALE = 2.0
BIG = 3e38

Q_RUNS = [(0, 0, 1), (1, 0, 1), (2, 0, 1), (3, 1, 1), (4, 1, 2)]
K_RUNS = [(0, 0, 3), (3, 0, 2), (5, 0, 1)]


class Count:

    def __init__(self, ctx, nc, name, per):
        self.sem = ctx.enter_context(nc.semaphore(name))
        self.per = per

    def at(self, pair, k):
        return pair * self.per + k


def later(pair):
    return not (isinstance(pair, int) and pair == 0)


def tile_cols(t):
    return slice(t * TR, t * TR + ROWS[t % 2])


def image_cols(b, lo=0, hi=TOK):
    return slice(2 * b * TR + lo, 2 * b * TR + hi)


def vit_tower(nc, x, w1, w2, lnp, wqkv1, wo1, wgl, wqkv2, wlora, wo2, ident, identb, masks, sel, marks, rank8, out):
    with ExitStack() as ctx:
        def sb(name, shape, dt=F32):
            return ctx.enter_context(nc.sbuf_tensor(name, shape, dt))

        def cnt(name, per):
            return Count(ctx, nc, name, per)

        def cnt2(name, per):
            return [Count(ctx, nc, f"{name}{s}", per) for s in range(2)]

        ps = ctx.enter_context(nc.psum_tensor("ps", [128, 8, 512], F32))
        dparts = [nc.dram_tensor(f"parts_dram{s}", (2, 2, PARTS, FC, PT), BF16, kind="Internal").ap() for s in range(2)]
        dmax = [nc.dram_tensor(f"max_dram{s}", (2, PARTS * HEADS, TOK), BF16, kind="Internal").ap() for s in range(2)]

        w1_s = sb("w1_s", [XR * 2 + 1, QH, D])
        w2_s = sb("w2_s", [FC + 2, 2, D])
        lnp_s = sb("lnp_s", [FC, 2, 2])
        wqkv_s = [sb("wqkv1_s", [FC, 2, 3 * D]), sb("wqkv2_s", [FC + 1 + EXPERTS, 2, 3 * D])]
        wlora_s = sb("wlora_s", [ER, 3 * D])
        wgl_s = sb("wgl_s", [FC + 1, 2, ER + EXPERTS])
        wo_s = [sb("wo1_s", [128, GROUPS, D]), sb("wo2_s", [128, GROUPS, D])]
        id_s = sb("id_s", [128, 128])
        idb_s = sb("idb_s", [128, 128], BF16)
        mask_s = sb("mask_s", [HALF + 1, 4, HALF + 1], BF16)
        sel_s = sb("sel_s", [128, 128])
        rank_s = sb("rank_s", [HALF + 1, EXPERTS])
        xb = sb("xb", [XR * 2 + 1, 2, GRID, IMG])
        h0n = sb("h0n", [HALF, 4, D])
        gT = sb("gT", [FC + 2, 2, PT])
        h1 = sb("h1", [HALF + 1, 4, D])
        h1k = sb("h1k", [HALF + 1, 4, D])
        n1 = sb("n1", [HALF + 1, 4, D])
        nT1 = sb("nT1", [FC, 2, PT])
        h2 = sb("h2", [HALF + 1, 4, D])
        h2k = sb("h2k", [HALF + 1, 4, D])
        n2 = sb("n2", [HALF + 1, 4, D])
        nT2 = sb("nT2", [FC + 1 + EXPERTS, 2, PT])
        hw = sb("hw", [HALF + 1, 4, ER])
        hwT = sb("hwT", [ER, PT])
        outb = sb("outb", [HALF + 1, 4, D])
        st = [sb(f"st{k}", [HALF + 1, 4, 6]) for k in range(3)]
        mv = [sb(f"mv{k}", [HALF + 1, 4, 2]) for k in range(3)]
        ve = [sb(f"ve{k}", [HALF + 1, 4, 1]) for k in range(3)]
        half_s = sb("half_s", [HALF + 1, 2, 1])
        rstd = [sb(f"rstd{k}", [HALF + 1, 4, 1]) for k in range(3)]
        parts = [sb(f"parts{s}", [FC, 4, PARTS, PT], BF16) for s in range(2)]
        rest = sb("rest", [FC, 4, PT])
        Qs = [sb(f"Qs{s}", [SR + PARTS, HEADS, PT], BF16) for s in range(2)]
        Ks = [sb(f"Ks{s}", [SR + PARTS, HEADS, PT], BF16) for s in range(2)]
        V = [sb(f"V{s}", [128, 4, HEADS, 32]) for s in range(2)]
        mx = sb("mx", [HALF + 1, 2, 2, HEADS])
        mxr = sb("mxr", [HALF + 1, 2, HEADS])
        mxp = sb("mxp", [HALF + 1, 2, 2, PARTS, HEADS], BF16)
        mT = sb("mT", [PARTS * HEADS, 2, TOK], BF16)
        P = sb("P", [128, 4, GH * TOK])
        O = [sb(f"O{s}", [128, GROUPS, PT]) for s in range(2)]
        inv = [[sb(f"inv{s}{g}", [128, PT]) for g in range(GROUPS)] for s in range(2)]
        lg = sb("lg", [HALF + 1, 4, EXPERTS])
        pe_ = sb("probs", [HALF + 1, 4, EXPERTS])
        pr = sb("pr", [HALF + 1, 4, EXPERTS])
        ge = sb("ge", [HALF + 1, 4, EXPERTS])
        gs = sb("gs", [HALF + 1, 4, ER + EXPERTS])
        gc = sb("gc", [HALF + 1, 4, EXPERTS])
        s1 = sb("s1", [HALF + 1, 4, EXPERTS])
        s2 = sb("s2", [HALF + 1, 4, EXPERTS])
        gm = sb("gm", [HALF + 1, 4, 1])
        gsum = sb("gsum", [HALF + 1, 4, 1])
        comb = sb("comb", [HALF + 1, 4, 1 + EXPERTS])

        weights_in = cnt("weights_in", 0)
        init_done = cnt("init_done", 0)
        wait_held = cnt("wait_held", 0)
        x_in = cnt("x_in", 12 * 16)
        patch_mm = cnt("patch_mm", 2)
        h0_normed = cnt("h0_normed", 2)
        h0T_mm = cnt("h0T_mm", 2)
        gelu_done = cnt("gelu_done", 4)
        w2_mm = cnt("w2_mm", 2)
        h1_copied = cnt("h1_copied", 2)
        n1_normed = cnt("n1_normed", 2)
        n1T_mm = cnt("n1T_mm", 2)
        n1T_copied = cnt("n1T_copied", 2)
        qk_mm = cnt2("qk_mm", 4)
        hi_done = cnt2("hi_done", 4)
        rest_done = cnt2("rest_done", 4)
        lo_done = cnt2("lo_done", 4)
        mid_done = cnt2("mid_done", 4)
        parts_out = [cnt2(f"parts_out{qk}", 2 * 16) for qk in "qk"]
        stacks_in = cnt2("stacks_in", 8 * 16)
        v_mm = cnt2("v_mm", 2)
        v_copied = cnt2("v_copied", 2)
        p1_mm = cnt2("p1_mm", 12)
        max_done = cnt2("max_done", 12)
        max_parts = cnt2("max_parts", 2)
        mT_mm = cnt2("mT_mm", 2)
        mT_copied = cnt2("mT_copied", 2)
        mT_out = cnt2("mT_out", 2 * 16)
        mT_in = [[cnt(f"mT_in{s}{b}", 16) for b in range(2)] for s in range(2)]
        p2_mm = cnt2("p2_mm", 12)
        exp_done = cnt2("exp_done", 12)
        av_mm = cnt2("av_mm", 6)
        av_copied = cnt2("av_copied", 6)
        sum_mm = cnt2("sum_mm", 3)
        inverted = cnt2("inverted", 3)
        divided = cnt2("divided", 3)
        wo_mm = cnt2("wo_mm", 2)
        added = cnt2("added", 2)
        n2_normed = cnt("n2_normed", 2)
        n2T_mm = cnt("n2T_mm", 2)
        n2T_copied = cnt("n2T_copied", 2)
        gate_mm = cnt("gate_mm", 2)
        gate_copied = cnt("gate_copied", 2)
        kept = cnt2("kept", 1)
        logits_done = cnt("logits_done", 1)
        gate_exp = cnt("gate_exp", 1)
        comb_done = cnt("comb_done", 1)
        hw_done = cnt("hw_done", 1)
        hwT_mm = cnt("hwT_mm", 1)
        hwT_copied = cnt("hwT_copied", 2)
        out_stored = cnt("out_stored", 6 * 16)
        dve_stats = [cnt(f"dve_stats{k}", 4) for k in range(3)]
        dve_here = cnt("dve_here", 12)
        dve_max = cnt2("dve_max", 2 * 3)
        var_done = [cnt(f"var_done{k}", 2) for k in range(3)]
        rstd_done = [cnt(f"rstd_done{k}", 2) for k in range(3)]

        LOADS = [(w1_s[:, :, :], w1), (w2_s[:, :, :], w2), (lnp_s[:, :, :], lnp), (wqkv_s[0][:, :, :], wqkv1),
                 (wo_s[0][:, :, :], wo1), (wgl_s[:, :, :], wgl), (wqkv_s[1][:, :, :], wqkv2), (wlora_s[:, :], wlora),
                 (wo_s[1][:, :, :], wo2), (id_s[:, :], ident), (idb_s[:, :], identb), (mask_s[:, :, :], masks),
                 (sel_s[:, :], sel), (rank_s[:, :], rank8)]
        N_INIT = 19

        def score_slot(z, n, lo, cols):
            return ps[0:n, 2 * z:2 * z + 2, 0:2 * TOK].rearrange("p k (h c) -> p k h c", h=2)[:, :, :, lo:lo + cols]

        block = ctx.enter_context(nc.Block())

        def hold_wait(eng):
            eng.sem_inc(wait_held.sem, 1)

        @block.sync
        def _(sp):
            def load_x(n):
                img = x.rearrange("b c (g p) w -> b c p g w", p=PATCH)
                for b in range(2):
                    for c in range(CHANNELS):
                        for s in range(2):
                            r = XR * s + PATCH * c
                            src = img[bass.ds(2 * n + b, 1), c].rearrange("o p g w -> (o p) g w")
                            sp.dma_start(xb[r:r + PATCH, b, :, 0:IMG - QH * s],
                                         src[:, :, QH * s:IMG]).then_inc(x_in.sem, 16)

            def part_out(s, n, m):
                if m == 0 and later(n):
                    sp.wait_ge(stacks_in[s].sem, stacks_in[s].at(n - 1, stacks_in[s].per))
                if m == 0:
                    hold_wait(sp)
                sp.wait_ge(lo_done[s].sem, lo_done[s].at(n, m + 1))
                sp.dma_start(dparts[s][m // 2, m % 2].rearrange("r p c -> p r c"),
                             parts[s][:, m, :, :]).then_inc(parts_out[m // 2][s].sem, 16)

            def stacks(s, n, qk):
                stack, runs = ((Qs[s], Q_RUNS), (Ks[s], K_RUNS))[qk]
                sp.wait_ge(parts_out[qk][s].sem, parts_out[qk][s].at(n, 2 * 16))
                if later(n):
                    sp.wait_ge(p2_mm[s].sem, p2_mm[s].at(n - 1, 12))
                for slot, part, k in runs:
                    src = dparts[s][qk].rearrange("m r (j h) c -> (r j) m h c", h=6)
                    sp.dma_start(stack[HD * slot:HD * (slot + k), :, :].rearrange("p (m h) c -> p m (h c)", m=2),
                                 src[HD * part:HD * (part + k)].rearrange("p m h c -> p m (h c)")).then_inc(stacks_in[s].sem, 16)

            def max_rows(s, n, b):
                sp.wait_ge(mT_copied[s].sem, mT_copied[s].at(n, b + 1))
                sp.dma_start(dmax[s][b], mT[:, b, :]).then_inc(mT_out[s].sem, 16)
                sp.wait_ge(mT_out[s].sem, mT_out[s].at(n, 16 * (b + 1)))
                sp.dma_start(Qs[s][SR:SR + PARTS, :, image_cols(b)],
                             dmax[s][b].rearrange("(r h) c -> r h c", r=PARTS)).then_inc(mT_in[s][b].sem, 16)

            def store(n):
                images = [out[bass.ds(sp.snap(2 * n + b), 1)].rearrange("o t d -> (o t) d") for b in range(2)]
                sp.wait_ge(added[1].sem, added[1].at(n, 2))
                for b, dst in enumerate(images):
                    sp.dma_start(dst[0:1], outb[HALF:HALF + 1, 2 * b, :]).then_inc(out_stored.sem, 16)
                    for a in range(2):
                        sp.dma_start(dst[1 + HALF * a:1 + HALF * (a + 1)],
                                     outb[0:HALF, 2 * b + a, :]).then_inc(out_stored.sem, 16)

            def body(i, done, att, load, emb):
                if att is not None:
                    max_rows(0, att, 0)
                if done is not None:
                    store(done)
                part_out(1, i, 0)
                part_out(1, i, 1)
                if att is not None:
                    max_rows(0, att, 1)
                stacks(1, i, 0)
                part_out(1, i, 2)
                part_out(1, i, 3)
                stacks(1, i, 1)
                if load is not None:
                    sp.wait_ge(patch_mm.sem, patch_mm.at(emb, 2))
                    load_x(load)
                max_rows(1, i, 0)
                max_rows(1, i, 1)
                if emb is not None:
                    for qk in range(2):
                        part_out(0, emb, 2 * qk)
                        part_out(0, emb, 2 * qk + 1)
                        stacks(0, emb, qk)

            for dst, src in LOADS:
                sp.dma_start(dst, src).then_inc(weights_in.sem, 16)
            sp.wait_ge(init_done.sem, N_INIT)
            sp.dma_start(gT[FC:FC + 2, 1, :], marks).then_inc(weights_in.sem, 16)
            load_x(0)
            for n in range(2):
                sp.wait_ge(patch_mm.sem, patch_mm.at(n, 2))
                load_x(n + 1)
                for qk in range(2):
                    part_out(0, n, 2 * qk)
                    part_out(0, n, 2 * qk + 1)
                    stacks(0, n, qk)
                if n == 0:
                    max_rows(0, 0, 0)
                    max_rows(0, 0, 1)
            body(0, None, 1, 3, 2)
            with sp.Fori(1, PAIRS - 3) as i:
                body(i, sp.snap(i - 1), sp.snap(i + 1), sp.snap(i + 3), sp.snap(i + 2))
            body(PAIRS - 3, PAIRS - 4, PAIRS - 2, None, PAIRS - 1)
            body(PAIRS - 2, PAIRS - 3, PAIRS - 1, None, None)
            body(PAIRS - 1, PAIRS - 2, None, None, None)
            store(PAIRS - 1)
            sp.wait_ge(out_stored.sem, out_stored.at(PAIRS - 1, out_stored.per))

        N_WEIGHTS = 16 * (len(LOADS) + 1)

        GROUP_ORDER = [(0, 0), (0, 1), (1, 0), (1, 1), (0, 2), (1, 2)]
        AV_OF_SUM = [3, 4, 6]
        AV_BANK = [[4, 5, 4, 5, 5, 5], [5, 4, 5, 5, 5, 5]]
        UNITS_BEFORE = [8, 12]

        @block.gpsimd
        def _(pool):
            fills = [(xb[:, :, :, :], 1.0), (gT[:, :, :], 0.0), (V[0][:, :, :, :], 0.0), (V[1][:, :, :, :], 0.0),
                     (mx[:, :, :, :], 0.0), (comb[:, :, :], 1.0), (O[0][:, :, :], 1.0), (O[1][:, :, :], 1.0),
                     (lg[:, :, :], 0.0), (ve[0][:, :, :], 1.0),
                     (ve[1][:, :, :], 1.0), (ve[2][:, :, :], 1.0), (half_s[:, :, :], -0.5),
                     (Ks[0][SR:SR + PARTS, :, :], 1.0), (Ks[1][SR:SR + PARTS, :, :], 1.0),
                     (nT2[:, :, :], 1.0), (P[:, :, :], 0.0),
                    
                     (V[0][:, :, :, HD:HD + 1], 1.0), (V[1][:, :, :, HD:HD + 1], 1.0)]
            assert len(fills) == N_INIT
            for k, (dst, value) in enumerate(fills):
                pool.memset(dst, value).then_inc(init_done.sem, 1)
                pool.wait_ge(init_done.sem, k + 1)

            def rsqrt(which, n, b, used):
                if later(n):
                    pool.wait_ge(used.sem, used.at(n - 1, b + 1))
                pool.wait_ge(var_done[which].sem, var_done[which].at(n, b + 1))
                pool.tensor_tensor(rstd[which][:, 2 * b:2 * b + 2, :], ve[which][:, 2 * b:2 * b + 2, :],
                                   half_s[:, 0:2, :], ALU.pow).then_inc(rstd_done[which].sem, 1)

            def cut(s, n, m):
                pool.wait_ge(rest_done[s].sem, rest_done[s].at(n, m + 1))
                hold_wait(pool)
                pool.tensor_copy(parts[s][:, m, 1, :], rest[:, m, :]).then_inc(mid_done[s].sem, 1)
                pool.wait_ge(mid_done[s].sem, mid_done[s].at(n, m + 1))
                pool.tensor_tensor(parts[s][:, m, 2, :], rest[:, m, :], parts[s][:, m, 1, :],
                                   ALU.subtract).then_inc(lo_done[s].sem, 1)

            def keep(s, n):
                if s == 0:
                    pool.wait_ge(h1_copied.sem, h1_copied.at(n, 2))
                else:
                    pool.wait_ge(added[0].sem, added[0].at(n, 2))
                if later(n):
                    pool.wait_ge(added[s].sem, added[s].at(n - 1, 2))
                hold_wait(pool)
                pool.tensor_copy((h1k, h2k)[s][:, :, :], (h1, h2)[s][:, :, :]).then_inc(kept[s].sem, 1)

            def divide(s, n, g):
                pool.wait_ge(inverted[s].sem, inverted[s].at(n, g + 1))
                hold_wait(pool)
                pool.tensor_tensor(O[s][:, g, :], O[s][:, g, :], inv[s][g][:, :], ALU.mult).then_inc(divided[s].sem, 1)

            def cut_chunks(s, n, chunks):
                for m in chunks:
                    cut(s, n, m)

            def body(i, done, att, emb):
                rsqrt(2, i, 0, n2_normed)
                rsqrt(2, i, 1, n2_normed)
                if done is not None:
                    divide(1, done, 2)
                if att is not None:
                    keep(0, att)
                cut_chunks(1, i, range(4))
                if att is not None:
                    divide(0, att, 0)
                if emb is not None:
                    rsqrt(0, emb, 0, h0_normed)
                if att is not None:
                    divide(0, att, 1)
                if emb is not None:
                    rsqrt(0, emb, 1, h0_normed)
                    rsqrt(1, emb, 0, n1_normed)
                keep(1, i)
                if emb is not None:
                    rsqrt(1, emb, 1, n1_normed)
                if att is not None:
                    divide(0, att, 2)
                if emb is not None:
                    cut_chunks(0, emb, range(3))
                divide(1, i, 0)
                if emb is not None:
                    cut_chunks(0, emb, [3])
                divide(1, i, 1)

            def embed(n):
                for which, used in ((0, h0_normed), (1, n1_normed)):
                    for b in range(2):
                        rsqrt(which, n, b, used)
                cut_chunks(0, n, range(4))

            embed(0)
            keep(0, 0)
            for g in range(GROUPS):
                divide(0, 0, g)
            embed(1)
            body(0, None, 1, 2)
            with pool.Fori(1, PAIRS - 2) as i:
                body(i, i - 1, i + 1, i + 2)
            body(PAIRS - 2, PAIRS - 3, PAIRS - 1, None)
            body(PAIRS - 1, PAIRS - 2, None, None)
            divide(1, PAIRS - 1, 2)

        @block.tensor
        def _(pe):

            def patch(n, b, a, reader):
                if b == 0 and a == 0:
                    pe.wait_ge(x_in.sem, x_in.at(n, x_in.per))
                if reader is not None:
                    pe.wait_ge(reader[0].sem, reader[0].at(reader[1], reader[2]))
                for q in range(QH):
                    k = 2 * XR + (q == 0)
                    mm = pe.matmul(ps[0:HALF, 6 + b, a * D:(a + 1) * D],
                                   xb[0:k, b, 7 * a:7 * a + 7, q:q + PATCH * (GRID - 1) + 1:PATCH],
                                   w1_s[0:k, q, :], start=(q == 0), stop=(q == QH - 1))
                if a == 1:
                    mm.then_inc(patch_mm.sem, 1)

            def turn_h0(n, b, reader):
                pe.wait_ge(h0_normed.sem, h0_normed.at(n, b + 1))
                if reader is not None:
                    pe.wait_ge(reader[0].sem, reader[0].at(reader[1], reader[2]))
                for c in range(2):
                    for a in range(2):
                        lo = 256 * c + a * HALF
                        mm = pe.transpose(ps[0:FC, 6 + b, lo:lo + HALF],
                                          h0n[:, 2 * b + a, c * FC:(c + 1) * FC], id_s[0:HALF, 0:HALF])
                mm.then_inc(h0T_mm.sem, 1)

            def second(n, b):
                pe.wait_ge(gelu_done.sem, gelu_done.at(n, 2 * b + 2))
                for a in range(2):
                    dst = ps[0:TR, 6 + b, a * D:(a + 1) * D]
                    cols = image_cols(b, a * TR, (a + 1) * TR)
                    pe.matmul(dst, gT[0:FC, 0, cols], w2_s[0:FC, 0, :], start=True, stop=False)
                    mm = pe.matmul(dst, gT[0:FC + 2, 1, cols], w2_s[0:FC + 2, 1, :], start=False, stop=True)
                mm.then_inc(w2_mm.sem, 1)

            def turn(src, b):
                for c in range(2):
                    for a in range(2):
                        lo = 256 * c + a * TR
                        mm = pe.transpose(ps[0:FC, 6 + b, lo:lo + TR], src[:, 2 * b + a, c * FC:(c + 1) * FC],
                                          id_s[0:TR, 0:TR])
                return mm

            def turn_n1(n, b):
                pe.wait_ge(n1_normed.sem, n1_normed.at(n, b + 1))
                pe.wait_ge(h1_copied.sem, h1_copied.at(n, b + 1))
                turn(n1, b).then_inc(n1T_mm.sem, 1)

            def qk1(n, m):
                if m == 0:
                    pe.wait_ge(n1T_copied.sem, n1T_copied.at(n, 2))
                if m >= 2:
                    pe.wait_ge(rest_done[0].sem, rest_done[0].at(n, m - 1))
                for c in range(2):
                    mm = pe.matmul(ps[0:FC, 6 + m % 2, 0:PT], wqkv_s[0][:, c, m * FC:(m + 1) * FC], nT1[:, c, :],
                                   start=(c == 0), stop=(c == 1))
                mm.then_inc(qk_mm[0].sem, 1)

            def v1(n, b):
                pe.wait_ge(rest_done[0].sem, rest_done[0].at(n, b + 3))
                for a in range(2):
                    for c in range(2):
                        mm = pe.matmul(ps[0:TR, 6 + b, a * D:(a + 1) * D], nT1[:, c, image_cols(b, a * TR, (a + 1) * TR)],
                                       wqkv_s[0][:, c, 2 * D:3 * D], start=(c == 0), stop=(c == 1))
                mm.then_inc(v_mm[0].sem, 1)

            def project(s, n, b, reader):
                pe.wait_ge(reader[0].sem, reader[0].at(reader[1], reader[2]))
                pe.wait_ge(divided[s].sem, divided[s].at(n, GROUPS))
                for a in range(2):
                    for g in range(GROUPS):
                        mm = pe.matmul(ps[0:TR, 6 + b, a * D:(a + 1) * D], O[s][:, g, image_cols(b, a * TR, (a + 1) * TR)],
                                       wo_s[s][:, g, :], start=(g == 0), stop=(g == GROUPS - 1))
                mm.then_inc(wo_mm[s].sem, 1)

            def turn_n2(n, b, reader):
                pe.wait_ge(n2_normed.sem, n2_normed.at(n, b + 1))
                pe.wait_ge(reader[0].sem, reader[0].at(reader[1], reader[2]))
                turn(n2, b).then_inc(n2T_mm.sem, 1)

            def gate(n, b):
                pe.wait_ge(n2T_copied.sem, n2T_copied.at(n, b + 1))
                for a in range(2):
                    cols = image_cols(b, a * TR, (a + 1) * TR)
                    dst = ps[0:TR, 6 + b, 256 * a:256 * a + ER + EXPERTS]
                    pe.matmul(dst, nT2[0:FC, 0, cols], wgl_s[0:FC, 0, :], start=True, stop=False)
                    mm = pe.matmul(dst, nT2[0:FC + 1, 1, cols], wgl_s[0:FC + 1, 1, :], start=False, stop=True)
                mm.then_inc(gate_mm.sem, 1)

            def turn_hw(n, reader):
                pe.wait_ge(hw_done.sem, hw_done.at(n, 1))
                if later(n):
                    pe.wait_ge(inverted[1].sem, inverted[1].at(n - 1, GROUPS))
                pe.wait_ge(reader[0].sem, reader[0].at(reader[1], reader[2]))
                for t in range(4):
                    pe.transpose(ps[0:ER, 4, t * TR:(t + 1) * TR], hw[:, t, :], id_s[0:TR, 0:TR])
                    mm = pe.transpose(ps[0:1 + EXPERTS, 5, t * TR:(t + 1) * TR], comb[:, t, :], id_s[0:TR, 0:TR])
                mm.then_inc(hwT_mm.sem, 1)

            def qk2_start(n, m, reader):
                pe.wait_ge(reader[0].sem, reader[0].at(reader[1], reader[2]))
                pe.matmul(ps[0:FC, 6 + m % 2, 0:PT], wqkv_s[1][0:FC, 0, m * FC:(m + 1) * FC], nT2[0:FC, 0, 0:PT],
                          start=True, stop=False)

            def qk2(n, m):
                if m == 0:
                    pe.wait_ge(hwT_copied.sem, hwT_copied.at(n, 2))
                dst = ps[0:FC, 6 + m % 2, 0:PT]
                cols = slice(m * FC, (m + 1) * FC)
                pe.matmul(dst, wqkv_s[1][:, 1, cols], nT2[:, 1, 0:PT], start=False, stop=False)
                pe.matmul(dst, wlora_s[:, cols], hwT[:, :], start=False, stop=True).then_inc(qk_mm[1].sem, 1)

            def v2(n, b, reader):
                pe.wait_ge(reader[0].sem, reader[0].at(reader[1], reader[2]))
                vcols = slice(2 * D, 3 * D)
                for a in range(2):
                    dst = ps[0:TR, 6 + b, a * D:(a + 1) * D]
                    cols = image_cols(b, a * TR, (a + 1) * TR)
                    pe.matmul(dst, nT2[0:FC, 0, cols], wqkv_s[1][0:FC, 0, vcols], start=True, stop=False)
                    pe.matmul(dst, nT2[:, 1, cols], wqkv_s[1][:, 1, vcols], start=False, stop=False)
                    mm = pe.matmul(dst, hwT[:, cols], wlora_s[:, vcols], start=False, stop=True)
                mm.then_inc(v_mm[1].sem, 1)

            def pass1(s, n, u, before):
                b, a, g = u // 6, u // 3 % 2, u % 3
                if u == 0:
                    pe.wait_ge(stacks_in[s].sem, stacks_in[s].at(n, stacks_in[s].per))
                if u - UNITS_BEFORE[s] in (0, 1):
                    pe.wait_ge(exp_done[s].sem, exp_done[s].at(n, u - UNITS_BEFORE[s] + 1))
                elif u >= 2:
                    pe.wait_ge(max_done[s].sem, max_done[s].at(n, u - 1))
                elif before is not None:
                    pe.wait_ge(exp_done[before[0]].sem, exp_done[before[0]].at(before[1], 11 + u))
                z, r = u % 2, ROWS[a]
                keys = ROWS[0] if (s == 0 and a == 0) else TOK
                for h in range(GH):
                    hd = GH * g + h
                    dst = ps[0:r, 2 * z + h // 2, (h % 2) * TOK:(h % 2) * TOK + keys]
                    mm = pe.matmul(dst, Qs[s][0:SR, hd, tile_cols(2 * b + a)],
                                   Ks[s][0:SR, hd, image_cols(b, 0, keys)], start=True, stop=(s == 1))
                    if s == 0:
                        c0 = (h % 2) * TOK + a * ROWS[0]
                        mm = pe.matmul(ps[0:r, 2 * z + h // 2, c0:c0 + r], idb_s[0:r, 0:r],
                                       mask_s[0:r, a, 0:r], start=False, stop=True)
                mm.then_inc(p1_mm[s].sem, 1)

            def turn_max(s, n, b, before):
                pe.wait_ge(max_parts[s].sem, max_parts[s].at(n, b + 1))
                if b == 1:
                    pe.wait_ge(mT_copied[s].sem, mT_copied[s].at(n, 1))
                elif before is not None:
                    pe.wait_ge(av_copied[before[0]].sem, av_copied[before[0]].at(before[1], 6))
                for a in range(2):
                    lo = b * TOK + a * TR
                    mm = pe.matmul(ps[0:PARTS * HEADS, 5, lo:lo + ROWS[a]],
                                   mxp[0:ROWS[a], b, a, :, :].rearrange("p r h -> p (r h)"), idb_s[0:ROWS[a], 0:ROWS[a]],
                                   start=True, stop=True)
                mm.then_inc(mT_mm[s].sem, 1)

            def pass2(s, n, v):
                b, g = GROUP_ORDER[v]
                if g == 0:
                    pe.wait_ge(mT_in[s][b].sem, mT_in[s][b].at(n, 16))
                for a in range(2):
                    u = 2 * v + a
                    if u < 2:
                        pe.wait_ge(max_done[s].sem, max_done[s].at(n, UNITS_BEFORE[s] - 1 + u))
                    elif u < 4 and UNITS_BEFORE[s] < 12:
                        pe.wait_ge(max_done[s].sem, max_done[s].at(n, 9 + u))
                    else:
                        pe.wait_ge(exp_done[s].sem, exp_done[s].at(n, u - 1))
                    z, r = u % 2, ROWS[a]
                    lo = ROWS[0] if (s == 0 and a == 1) else 0
                    for h in range(GH):
                        hd = GH * g + h
                        c0 = (h % 2) * TOK
                        mm = pe.matmul(ps[0:r, 2 * z + h // 2, c0 + lo:c0 + TOK],
                                       Ks[s][0:SR + PARTS, hd, tile_cols(2 * b + a)],
                                       Qs[s][0:SR + PARTS, hd, image_cols(b, lo)], start=True, stop=(s == 1))
                        if s == 0:
                            c0 += a * ROWS[0]
                            mm = pe.matmul(ps[0:r, 2 * z + h // 2, c0:c0 + r], idb_s[0:r, 0:r],
                                           mask_s[0:r, 2 + a, 0:r], start=False, stop=True)
                    mm.then_inc(p2_mm[s].sem, 1)

            def av(s, n, v, before=None):
                b, g = GROUP_ORDER[v]
                if v == 0:
                    pe.wait_ge(v_copied[s].sem, v_copied[s].at(n, 2))
                pe.wait_ge(exp_done[s].sem, exp_done[s].at(n, 2 * v + 2))
                if v == 1 - s:
                    pe.wait_ge(mT_copied[s].sem, mT_copied[s].at(n, 2))
                elif v == s:
                    if before is not None:
                        pe.wait_ge(inverted[before[0]].sem, inverted[before[0]].at(before[1], GROUPS))
                else:
                    pe.wait_ge(av_copied[s].sem, av_copied[s].at(n, v if v >= 4 - s else v - 1))
                bank = AV_BANK[s][v]
                for a in range(2):
                    lo = ROWS[0] if (s == 0 and a == 1) else 0
                    for h in range(GH):
                        mm = pe.matmul(ps[32 * h:32 * h + 32, bank, lo:TOK],
                                       V[s][:, 2 * b + a, GH * g + h, :],
                                       P[:, (2 * v + a) % 4, h * TOK + lo:(h + 1) * TOK],
                                       start=(a == 0), stop=(a == 1))
                mm.then_inc(av_mm[s].sem, 1)

            def sums(s, n, g):
                pe.wait_ge(av_copied[s].sem, av_copied[s].at(n, AV_OF_SUM[g]))
                if g >= 1:
                    pe.wait_ge(inverted[s].sem, inverted[s].at(n, g))
                pe.matmul(ps[:, 4, 0:PT], sel_s[:, :], O[s][:, g, :], start=True, stop=True).then_inc(sum_mm[s].sem, 1)

            def embed(n, last):
                for b in range(2):
                    patch(n, b, 0, (v_copied[0], last, b + 1) if last is not None else None)
                    patch(n, b, 1, None)
                for b in range(2):
                    turn_h0(n, b, None)
                for b in range(2):
                    second(n, b)
                for b in range(2):
                    turn_n1(n, b)
                for m in range(4):
                    qk1(n, m)
                for b in range(2):
                    v1(n, b)

            def first_attention(n):
                for u in range(8):
                    pass1(0, n, u, None)
                turn_max(0, n, 0, None)
                pass2(0, n, 0)
                for u in range(8, 12):
                    pass1(0, n, u, None)
                turn_max(0, n, 1, None)
                av(0, n, 0)
                pass2(0, n, 1)
                for v in range(2, 6):
                    pass2(0, n, v)
                    av(0, n, v - 1)
                    if v >= 4:
                        sums(0, n, v - 4)
                av(0, n, 5)
                sums(0, n, 2)

            def body(i, done, att, emb, last):
                def p1(stage, *args):
                    if done is not None:
                        stage(1, done, *args)

                def a0(stage, *args):
                    if att is not None:
                        stage(0, att, *args)

                def d1(stage, *args):
                    if emb is not None:
                        stage(emb, *args)

                e0 = (1, i - 1) if done is not None else None
                e1 = (0, att) if att is not None else (1, i - 1)

                project(0, i, 0, (last[0], last[1], 1))
                p1(sums, 2)
                if done is not None and att is not None:
                    v1(att, 1)
                project(0, i, 1, (last[0], last[1], 2))
                a0(pass1, 0, e0)
                a0(pass1, 1, e0)
                turn_n2(i, 0, (added[0], i, 1))
                a0(pass1, 2, e0)
                turn_n2(i, 1, (added[0], i, 2))
                a0(pass1, 3, e0)
                gate(i, 0)
                a0(pass1, 4, e0)
                gate(i, 1)
                a0(pass1, 5, e0)
                p1(project, 0, (gate_copied, i, 1))
                a0(turn_max, 0, e0)
                p1(project, 1, (gate_copied, i, 2))
                a0(pass1, 6, e0)
                qk2_start(i, 0, (added[1], done, 1) if done is not None else (gate_copied, i, 1))
                qk2_start(i, 1, (added[1], done, 2) if done is not None else (gate_copied, i, 2))
                a0(pass1, 7, e0)
                turn_hw(i, (mT_copied[0], att, 1) if att is not None else (av_copied[1], i - 1, 6))
                a0(pass2, 0)
                qk2(i, 0)
                a0(av, 0, e0)
                a0(pass1, 8, e0)
                a0(pass1, 9, e0)
                qk2(i, 1)
                a0(pass1, 10, e0)
                a0(pass1, 11, e0)
                qk2_start(i, 2, (rest_done[1], i, 1))
                qk2(i, 2)
                a0(pass2, 1)
                a0(turn_max, 1, e0)
                qk2_start(i, 3, (rest_done[1], i, 2))
                qk2(i, 3)
                a0(av, 1)
                d1(patch, 0, 0, (rest_done[1], i, 3))
                a0(pass2, 2)
                a0(pass2, 3)
                a0(av, 2)
                a0(pass2, 4)
                a0(sums, 0)
                a0(av, 3)
                d1(patch, 0, 1, None)
                a0(pass2, 5)
                a0(av, 4)
                a0(sums, 1)
                d1(patch, 1, 0, (rest_done[1], i, 4))
                a0(av, 5)
                pass1(1, i, 0, e1)
                pass1(1, i, 1, e1)
                v2(i, 0, (h0_normed, emb, 1) if emb is not None else (rest_done[1], i, 3))
                pass1(1, i, 2, e1)
                d1(patch, 1, 1, None)
                d1(turn_h0, 0, (v_copied[1], i, 1))
                pass1(1, i, 3, e1)
                pass1(1, i, 4, e1)
                d1(second, 0)
                a0(sums, 2)
                pass1(1, i, 5, e1)
                v2(i, 1, (h0_normed, emb, 2) if emb is not None else (rest_done[1], i, 4))
                pass1(1, i, 6, e1)
                d1(turn_h0, 1, (v_copied[1], i, 2))
                turn_max(1, i, 0, e1)
                pass1(1, i, 7, e1)
                pass1(1, i, 8, e1)
                d1(second, 1)
                pass1(1, i, 9, e1)
                pass1(1, i, 10, e1)
                pass1(1, i, 11, e1)
                d1(turn_n1, 0)
                pass2(1, i, 0)
                turn_max(1, i, 1, e1)
                d1(turn_n1, 1)
                pass2(1, i, 1)
                av(1, i, 0)
                d1(qk1, 0)
                pass2(1, i, 2)
                av(1, i, 1, e1)
                d1(qk1, 1)
                pass2(1, i, 3)
                av(1, i, 2)
                d1(qk1, 2)
                sums(1, i, 0)
                pass2(1, i, 4)
                av(1, i, 3)
                d1(qk1, 3)
                pass2(1, i, 5)
                sums(1, i, 1)
                av(1, i, 4)
                d1(v1, 0)
                av(1, i, 5)

            pe.wait_ge(weights_in.sem, N_WEIGHTS)
            pe.wait_ge(init_done.sem, N_INIT)
            embed(0, None)
            first_attention(0)
            embed(1, 0)
            body(0, None, 1, 2, (v_copied[0], 1))
            with pe.Fori(1, PAIRS - 2) as i:
                body(i, i - 1, i + 1, i + 2, (v_copied[0], i + 1))
            body(PAIRS - 2, PAIRS - 3, PAIRS - 1, None, (v_copied[0], PAIRS - 1))
            body(PAIRS - 1, PAIRS - 2, None, None, (v_copied[1], PAIRS - 2))
            sums(1, PAIRS - 1, 2)
            for b in range(2):
                project(1, PAIRS - 1, b, (v_copied[1], PAIRS - 1, b + 1))

        @block.scalar
        def _(act):
            def gelu(n, b):
                act.wait_ge(h0T_mm.sem, h0T_mm.at(n, b + 1))
                if later(n):
                    act.wait_ge(w2_mm.sem, w2_mm.at(n - 1, b + 1))
                for c in range(2):
                    dst = gT[0:FC, c, image_cols(b, 0, 2 * TR)].rearrange("p (a k) -> p a k", a=2)[:, :, 0:HALF]
                    src = ps[0:FC, 6 + b, 256 * c:256 * c + 2 * HALF].rearrange("p (a k) -> p a k", a=2)
                    nc.scalar.activation(dst, src, ACT.Gelu, bias=lnp_s[:, c, 1:2],
                                         scale=lnp_s[:, c, 0:1]).then_inc(gelu_done.sem, 1)

            def copy_h1(n, b):
                act.wait_ge(w2_mm.sem, w2_mm.at(n, b + 1))
                if b == 0 and later(n):
                    act.wait_ge(kept[0].sem, kept[0].at(n - 1, 1))
                    act.wait_ge(n1_normed.sem, n1_normed.at(n - 1, 2))
                nc.scalar.activation(h1[:, 2 * b:2 * b + 2, :], ps[0:TR, 6 + b, 0:2 * D].rearrange("p (a d) -> p a d", a=2),
                                     ACT.Copy).then_inc(h1_copied.sem, 1)

            def copy_nT1(n, b):
                act.wait_ge(n1T_mm.sem, n1T_mm.at(n, b + 1))
                if b == 0 and later(n):
                    act.wait_ge(v_mm[0].sem, v_mm[0].at(n - 1, 2))
                src = ps[0:FC, 6 + b, :].rearrange("p (c k) -> p c k", c=2)[:, :, 0:2 * TR]
                nc.scalar.activation(nT1[:, :, image_cols(b, 0, 2 * TR)], src, ACT.Copy).then_inc(n1T_copied.sem, 1)

            def high(s, n, m):
                if m == 0 and later(n):
                    act.wait_ge(parts_out[0][s].sem, parts_out[0][s].at(n - 1, 2 * 16))
                    act.wait_ge(parts_out[1][s].sem, parts_out[1][s].at(n - 1, 2 * 16))
                act.wait_ge(qk_mm[s].sem, qk_mm[s].at(n, m + 1))
                nc.scalar.activation(parts[s][:, m, 0, :], ps[0:FC, 6 + m % 2, 0:PT], ACT.Copy).then_inc(hi_done[s].sem, 1)

            def copy_v(s, n, b):
                act.wait_ge(v_mm[s].sem, v_mm[s].at(n, b + 1))
                if b == 0 and later(n):
                    act.wait_ge(av_mm[s].sem, av_mm[s].at(n - 1, 6))
                nc.scalar.activation(V[s][0:TR, 2 * b:2 * b + 2, :, 0:HD],
                                     ps[0:TR, 6 + b, 0:2 * D].rearrange("p (a h d) -> p a h d", a=2, d=HD),
                                     ACT.Copy).then_inc(v_copied[s].sem, 1)

            def copy_mT(s, n, b, before):
                act.wait_ge(mT_mm[s].sem, mT_mm[s].at(n, b + 1))
                if b == 0 and before is not None:
                    act.wait_ge(mT_out[before[0]].sem, mT_out[before[0]].at(before[1], 32))
                nc.scalar.activation(mT[:, b, :], ps[0:PARTS * HEADS, 5, b * TOK:(b + 1) * TOK],
                                     ACT.Copy).then_inc(mT_copied[s].sem, 1)

            def copy_av(s, n, v):
                b, g = GROUP_ORDER[v]
                act.wait_ge(av_mm[s].sem, av_mm[s].at(n, v + 1))
                if v == 0 and later(n):
                    act.wait_ge(wo_mm[s].sem, wo_mm[s].at(n - 1, 2))
                nc.scalar.activation(O[s][:, g, image_cols(b)], ps[:, AV_BANK[s][v], 0:TOK],
                                     ACT.Copy).then_inc(av_copied[s].sem, 1)

            def exps(s, n, v):
                for a in range(2):
                    u = 2 * v + a
                    act.wait_ge(p2_mm[s].sem, p2_mm[s].at(n, u + 1))
                    if u >= 4:
                        act.wait_ge(av_mm[s].sem, av_mm[s].at(n, v - 1))
                    lo = ROWS[0] if (s == 0 and a == 1) else 0
                    dst = P[0:ROWS[a], u % 4, :].rearrange("p (k h c) -> p k h c", k=2, h=2)[:, :, :, lo:TOK]
                    nc.scalar.activation(dst, score_slot(u % 2, ROWS[a], lo, TOK - lo), ACT.Exp,
                                         scale=SCALE).then_inc(exp_done[s].sem, 1)

            def copy_nT2(n, b):
                act.wait_ge(n2T_mm.sem, n2T_mm.at(n, b + 1))
                if b == 0 and later(n):
                    act.wait_ge(v_mm[1].sem, v_mm[1].at(n - 1, 2))
                src = ps[0:FC, 6 + b, :].rearrange("p (c k) -> p c k", c=2)[:, :, 0:2 * TR]
                nc.scalar.activation(nT2[0:FC, :, image_cols(b, 0, 2 * TR)], src, ACT.Copy).then_inc(n2T_copied.sem, 1)

            def copy_gate(n, b):
                act.wait_ge(gate_mm.sem, gate_mm.at(n, b + 1))
                src = ps[0:TR, 6 + b, :].rearrange("p (a k) -> p a k", a=2)[:, :, 0:ER + EXPERTS]
                nc.scalar.activation(gs[:, 2 * b:2 * b + 2, :], src, ACT.Copy).then_inc(gate_copied.sem, 1)

            def gate_exps(n):
                act.wait_ge(logits_done.sem, logits_done.at(n, 1))
                nc.scalar.activation(pe_[:, :, :], lg[:, :, :], ACT.Exp).then_inc(gate_exp.sem, 1)

            def copy_hwT(n):
                act.wait_ge(hwT_mm.sem, hwT_mm.at(n, 1))
                nc.scalar.activation(hwT[:, :], ps[0:ER, 4, 0:PT], ACT.Copy).then_inc(hwT_copied.sem, 1)
                nc.scalar.activation(nT2[FC:FC + 1 + EXPERTS, 1, :], ps[0:1 + EXPERTS, 5, 0:PT],
                                     ACT.Copy).then_inc(hwT_copied.sem, 1)

            def embed(n):
                for stage in (gelu, copy_h1, copy_nT1):
                    for b in range(2):
                        stage(n, b)
                for m in range(4):
                    high(0, n, m)
                for b in range(2):
                    copy_v(0, n, b)

            def first_attention(n):
                copy_mT(0, n, 0, None)
                exps(0, n, 0)
                copy_mT(0, n, 1, None)
                copy_av(0, n, 0)
                exps(0, n, 1)
                for v in range(2, 6):
                    exps(0, n, v)
                    copy_av(0, n, v - 1)
                copy_av(0, n, 5)

            def body(i, done, att, emb):
                def a0(stage, *args):
                    if att is not None:
                        stage(0, att, *args)

                def d1(stage, *args):
                    if emb is not None:
                        stage(*args)

                m0 = (1, i - 1) if done is not None else (0, 0)
                m1 = (0, att) if att is not None else (1, i - 1)
                if done is not None:
                    a0(copy_v, 1)
                copy_nT2(i, 0)
                copy_nT2(i, 1)
                copy_gate(i, 0)
                copy_gate(i, 1)
                gate_exps(i)
                a0(copy_mT, 0, m0)
                copy_hwT(i)
                a0(exps, 0)
                high(1, i, 0)
                a0(copy_av, 0)
                high(1, i, 1)
                high(1, i, 2)
                a0(exps, 1)
                a0(copy_mT, 1, m0)
                high(1, i, 3)
                a0(copy_av, 1)
                a0(exps, 2)
                a0(exps, 3)
                a0(copy_av, 2)
                a0(exps, 4)
                a0(copy_av, 3)
                a0(exps, 5)
                a0(copy_av, 4)
                a0(copy_av, 5)
                copy_v(1, i, 0)
                d1(gelu, emb, 0)
                d1(copy_h1, emb, 0)
                copy_v(1, i, 1)
                d1(gelu, emb, 1)
                copy_mT(1, i, 0, m1)
                d1(copy_h1, emb, 1)
                d1(copy_nT1, emb, 0)
                exps(1, i, 0)
                copy_mT(1, i, 1, m1)
                d1(copy_nT1, emb, 1)
                exps(1, i, 1)
                copy_av(1, i, 0)
                d1(high, 0, emb, 0)
                exps(1, i, 2)
                copy_av(1, i, 1)
                d1(high, 0, emb, 1)
                exps(1, i, 3)
                copy_av(1, i, 2)
                d1(high, 0, emb, 2)
                exps(1, i, 4)
                copy_av(1, i, 3)
                d1(high, 0, emb, 3)
                exps(1, i, 5)
                copy_av(1, i, 4)
                d1(copy_v, 0, emb, 0)
                copy_av(1, i, 5)

            act.wait_ge(weights_in.sem, N_WEIGHTS)
            act.wait_ge(init_done.sem, N_INIT)
            embed(0)
            first_attention(0)
            embed(1)
            body(0, None, 1, 2)
            with act.Fori(1, PAIRS - 2) as i:
                body(i, i - 1, i + 1, i + 2)
            body(PAIRS - 2, PAIRS - 3, PAIRS - 1, None)
            body(PAIRS - 1, PAIRS - 2, None, None)

        @block.vector
        def _(dve):
            at = {}

            def reset():
                for chain in (dve_here, *dve_stats, *dve_max):
                    at[chain] = 0

            def link(chain, n, ins):
                ins.then_inc(chain.sem, 1)
                at[chain] += 1
                dve.wait_ge(chain.sem, chain.at(n, at[chain]))

            def moments(which, n, b, r, srcs):
                for a in range(2):
                    last = dve.bn_stats(st[which][0:r, 2 * b + a, :], srcs[a])
                link(dve_stats[which], n, last)
                hold_wait(dve)
                for a in range(2):
                    last = dve.bn_aggr(mv[which][0:r, 2 * b + a, :], st[which][0:r, 2 * b + a, :])
                link(dve_stats[which], n, last)
                dve.tensor_scalar(ve[which][0:r, 2 * b:2 * b + 2, :], mv[which][0:r, 2 * b:2 * b + 2, 1:2], EPS, None,
                                  ALU.add).then_inc(var_done[which].sem, 1)

            def stats_h0(n, b):
                dve.wait_ge(patch_mm.sem, patch_mm.at(n, b + 1))
                moments(0, n, b, HALF, [ps[0:HALF, 6 + b, a * D:(a + 1) * D] for a in range(2)])

            def scale(which, n, b, dst, r, srcs, done):
                dve.wait_ge(rstd_done[which].sem, rstd_done[which].at(n, b + 1))
                for a in range(2):
                    t = 2 * b + a
                    last = dve.tensor_scalar(dst[:, t, :], srcs[a], mv[which][0:r, t, 0:1], rstd[which][0:r, t, :],
                                             ALU.subtract, ALU.mult)
                last.then_inc(done.sem, 1)

            def norm_h0(n, b):
                if b == 0 and later(n):
                    dve.wait_ge(h0T_mm.sem, h0T_mm.at(n - 1, 2))
                scale(0, n, b, h0n, HALF, [ps[0:HALF, 6 + b, a * D:(a + 1) * D] for a in range(2)], h0_normed)

            def norm_n1(n, b):
                if b == 0 and later(n):
                    dve.wait_ge(n1T_mm.sem, n1T_mm.at(n - 1, 2))
                scale(1, n, b, n1, TR, [h1[:, 2 * b + a, :] for a in range(2)], n1_normed)

            def norm_n2(n, b):
                if b == 0 and later(n):
                    dve.wait_ge(n2T_mm.sem, n2T_mm.at(n - 1, 2))
                scale(2, n, b, n2, TR, [h2[:, 2 * b + a, :] for a in range(2)], n2_normed)

            def stats_n1(n, b):
                dve.wait_ge(h1_copied.sem, h1_copied.at(n, b + 1))
                moments(1, n, b, TR, [h1[:, 2 * b + a, :] for a in range(2)])

            def stats_n2(n, b):
                dve.wait_ge(added[0].sem, added[0].at(n, b + 1))
                moments(2, n, b, TR, [h2[:, 2 * b + a, :] for a in range(2)])

            def remainder(s, n, m, before):
                dve.wait_ge(hi_done[s].sem, hi_done[s].at(n, m + 1))
                if before is not None:
                    dve.wait_ge(lo_done[before[0]].sem, lo_done[before[0]].at(before[1], m + 1))
                dve.tensor_tensor(rest[:, m, :], ps[0:FC, 6 + m % 2, 0:PT], parts[s][:, m, 0, :],
                                  ALU.subtract).then_inc(rest_done[s].sem, 1)

            def maximum(s, n, u):
                b, a, g = u // 6, u // 3 % 2, u % 3
                keys = ROWS[0] if (s == 0 and a == 0) else TOK
                dve.wait_ge(p1_mm[s].sem, p1_mm[s].at(n, u + 1))
                dve.tensor_reduce(mx[0:ROWS[a], b, a, GH * g:GH * (g + 1)].rearrange("p (k h) -> p k h", k=2),
                                  score_slot(u % 2, ROWS[a], 0, keys), AX_X, ALU.max).then_inc(max_done[s].sem, 1)

            def max_cut(s, n, b, before):
                dve.wait_ge(max_done[s].sem, max_done[s].at(n, 6 * b + 6))
                if before is not None:
                    dve.wait_ge(mT_mm[before[0]].sem, mT_mm[before[0]].at(before[1], 2))
                m, p = mx[:, b], mxp[:, b]
                link(dve_max[s], n, dve.tensor_scalar(p[:, :, 0, :], m, -1.0, None, ALU.mult))
                link(dve_max[s], n, dve.scalar_tensor_tensor(out=mxr[:, :, :], in0=m, scalar=-1.0, in1=p[:, :, 0, :],
                                                             op0=ALU.mult, op1=ALU.subtract))
                link(dve_max[s], n, dve.tensor_copy(p[:, :, 1, :], mxr[:, :, :]))
                dve.tensor_tensor(p[:, :, 2, :], mxr[:, :, :], p[:, :, 1, :], ALU.subtract).then_inc(max_parts[s].sem, 1)

            def invert(s, n, g):
                dve.wait_ge(sum_mm[s].sem, sum_mm[s].at(n, g + 1))
                if later(n):
                    dve.wait_ge(divided[s].sem, divided[s].at(n - 1, g + 1))
                dve.reciprocal(inv[s][g][:, :], ps[:, 4, 0:PT]).then_inc(inverted[s].sem, 1)

            def add(s, n, b):
                res, dst = (h1k, h2) if s == 0 else (h2k, outb)
                if b == 0:
                    dve.wait_ge(kept[s].sem, kept[s].at(n, 1))
                if s == 0 and b == 0 and later(n):
                    dve.wait_ge(kept[1].sem, kept[1].at(n - 1, 1))
                if s == 1 and b == 0 and later(n):
                    dve.wait_ge(out_stored.sem, out_stored.at(n - 1, out_stored.per))
                dve.wait_ge(wo_mm[s].sem, wo_mm[s].at(n, b + 1))
                dve.tensor_tensor(dst[:, 2 * b:2 * b + 2, :], ps[0:TR, 6 + b, 0:2 * D].rearrange("p (a d) -> p a d", a=2),
                                  res[:, 2 * b:2 * b + 2, :], ALU.add).then_inc(added[s].sem, 1)

            def choose(n, done):
                def bc(ap):
                    return ap.to_broadcast([HALF + 1, 4, EXPERTS])

                rk = rank_s[:, :].unsqueeze(1).to_broadcast([HALF + 1, 4, EXPERTS])
                logits = gs[:, :, ER:ER + EXPERTS]
                dve.wait_ge(gate_copied.sem, gate_copied.at(n, 2))
                link(dve_here, n, dve.tensor_reduce(gm[:, :, 0], logits, AX_X, ALU.max))
                dve.tensor_tensor(lg[:, :, :], logits, bc(gm[:, :, :]), ALU.subtract).then_inc(logits_done.sem, 1)
                dve.wait_ge(logits_done.sem, logits_done.at(n, 1))
                link(dve_here, n, dve.scalar_tensor_tensor(out=gc[:, :, :], in0=lg[:, :, :], scalar=0.0, in1=rk,
                                                           op0=ALU.is_equal, op1=ALU.mult))
                link(dve_here, n, dve.tensor_reduce(gm[:, :, 0], gc[:, :, :], AX_X, ALU.max))
                link(dve_here, n, dve.tensor_tensor(s1[:, :, :], gc[:, :, :], bc(gm[:, :, :]), ALU.is_equal))
                link(dve_here, n, dve.scalar_tensor_tensor(out=pr[:, :, :], in0=s1[:, :, :], scalar=-BIG,
                                                           in1=lg[:, :, :], op0=ALU.mult, op1=ALU.add))
                link(dve_here, n, dve.tensor_reduce(gm[:, :, 0], pr[:, :, :], AX_X, ALU.max))
                link(dve_here, n, dve.tensor_tensor(ge[:, :, :], pr[:, :, :], bc(gm[:, :, :]), ALU.is_equal))
                link(dve_here, n, dve.tensor_tensor(gc[:, :, :], ge[:, :, :], rk, ALU.mult))
                if done is not None:
                    add(1, done, 0)
                    add(1, done, 1)
                dve.wait_ge(gate_exp.sem, gate_exp.at(n, 1))
                dve.tensor_reduce(gsum[:, :, 0], pe_[:, :, :], AX_X, ALU.add)
                link(dve_here, n, dve.tensor_reduce(gm[:, :, 0], gc[:, :, :], AX_X, ALU.max))
                dve.reciprocal(gsum[:, :, :], gsum[:, :, :])
                link(dve_here, n, dve.tensor_tensor(s2[:, :, :], gc[:, :, :], bc(gm[:, :, :]), ALU.is_equal))
                link(dve_here, n, dve.tensor_tensor(ge[:, :, :], s1[:, :, :], s2[:, :, :], ALU.add))
                link(dve_here, n, dve.scalar_tensor_tensor(out=pr[:, :, :], in0=pe_[:, :, :], scalar=LORA_SCALE,
                                                           in1=ge[:, :, :], op0=ALU.mult, op1=ALU.mult))
                dve.tensor_tensor(comb[:, :, 1:1 + EXPERTS], pr[:, :, :], bc(gsum[:, :, :]),
                                  ALU.mult).then_inc(comb_done.sem, 1)
                dve.wait_ge(comb_done.sem, comb_done.at(n, 1))
                dve.tensor_tensor(hw[:, :, :].rearrange("p t (e k) -> p t e k", e=EXPERTS),
                                  gs[:, :, 0:ER].rearrange("p t (e k) -> p t e k", e=EXPERTS),
                                  comb[:, :, 1:1 + EXPERTS].unsqueeze(3).to_broadcast([HALF + 1, 4, EXPERTS, RANK]),
                                  ALU.mult).then_inc(hw_done.sem, 1)

            def embed(n, before):
                for b in range(2):
                    stats_h0(n, b)
                for b in range(2):
                    norm_h0(n, b)
                for b in range(2):
                    stats_n1(n, b)
                for b in range(2):
                    norm_n1(n, b)
                for m in range(4):
                    remainder(0, n, m, before)

            def body(i, done, att, emb):
                def a0(stage, *args):
                    if att is not None:
                        stage(0, att, *args)

                def d1(stage, *args):
                    if emb is not None:
                        stage(*args)

                m0 = (1, i - 1) if done is not None else (0, 0)
                m1 = (0, att) if att is not None else (1, i - 1)
                r1 = (0, att) if att is not None else (1, i - 1)
                reset()
                add(0, i, 0)
                stats_n2(i, 0)
                norm_n2(i, 0)
                add(0, i, 1)
                stats_n2(i, 1)
                a0(maximum, 0)
                norm_n2(i, 1)
                a0(maximum, 1)
                a0(maximum, 2)
                if done is not None:
                    invert(1, done, 2)
                a0(maximum, 3)
                a0(maximum, 4)
                a0(maximum, 5)
                a0(max_cut, 0, m0)
                choose(i, done)
                a0(maximum, 6)
                a0(maximum, 7)
                a0(maximum, 8)
                remainder(1, i, 0, r1)
                a0(maximum, 9)
                a0(maximum, 10)
                remainder(1, i, 1, r1)
                a0(maximum, 11)
                a0(max_cut, 1, m0)
                remainder(1, i, 2, r1)
                remainder(1, i, 3, r1)
                a0(invert, 0)
                d1(stats_h0, emb, 0)
                d1(norm_h0, emb, 0)
                a0(invert, 1)
                maximum(1, i, 0)
                maximum(1, i, 1)
                maximum(1, i, 2)
                d1(stats_h0, emb, 1)
                maximum(1, i, 3)
                d1(norm_h0, emb, 1)
                maximum(1, i, 4)
                maximum(1, i, 5)
                max_cut(1, i, 0, m1)
                d1(stats_n1, emb, 0)
                maximum(1, i, 6)
                d1(norm_n1, emb, 0)
                maximum(1, i, 7)
                maximum(1, i, 8)
                maximum(1, i, 9)
                d1(stats_n1, emb, 1)
                maximum(1, i, 10)
                d1(norm_n1, emb, 1)
                maximum(1, i, 11)
                max_cut(1, i, 1, m1)
                a0(invert, 2)
                d1(remainder, 0, emb, 0, (1, i))
                d1(remainder, 0, emb, 1, (1, i))
                d1(remainder, 0, emb, 2, (1, i))
                invert(1, i, 0)
                d1(remainder, 0, emb, 3, (1, i))
                invert(1, i, 1)

                for chain in (dve_here, dve_max[1]):
                    assert at[chain] == chain.per, (chain.per, at[chain])

            dve.wait_ge(weights_in.sem, N_WEIGHTS)
            dve.wait_ge(init_done.sem, N_INIT)
            reset()
            embed(0, None)
            for u in range(12):
                maximum(0, 0, u)
                if u % 6 == 5:
                    max_cut(0, 0, u // 6, None)
            for g in range(GROUPS):
                invert(0, 0, g)
            reset()
            embed(1, (0, 0))
            body(0, None, 1, 2)
            with dve.Fori(1, PAIRS - 2) as i:
                body(i, i - 1, i + 1, i + 2)
            body(PAIRS - 2, PAIRS - 3, PAIRS - 1, None)
            body(PAIRS - 1, PAIRS - 2, None, None)
            invert(1, PAIRS - 1, 2)
            for b in range(2):
                add(1, PAIRS - 1, b)


def kernel(x, cls_tok, L0_tok_W1, L0_tok_b1, L0_tok_ln_w, L0_tok_ln_b, L0_tok_W2, L0_tok_b2,
           L0_attn_wq, L0_attn_wk, L0_attn_wv, L0_attn_wo, L0_ffn_Wg, L0_ffn_bg, L0_ffn_Wqkv, L0_ffn_bqkv,
           L0_ffn_Wproj, L0_ffn_bproj, L0_ffn_A, L0_ffn_ba, L0_ffn_Bm, L0_ffn_bb):
    import numpy as np
    import concourse.bacc as bacc
    from concourse.bass_utils import run_bass_kernel_spmd

    f = np.float32

    def zeros(*shape):
        return np.zeros(shape, f)

    order = np.array([(6 * m + h) * HD + j for m in range(2) for j in range(HD) for h in range(6)])

    def qkv_cols(wt):
        return np.concatenate([wt[:, 0:D][:, order], wt[:, D:2 * D][:, order], wt[:, 2 * D:]], axis=1)

    w1 = zeros(2 * XR + 1, QH, D)
    for s in range(2):
        w1[XR * s:XR * (s + 1)] = L0_tok_W1.reshape(XR, PATCH, D)[:, QH * s:QH * (s + 1)]
    w1[2 * XR, 0] = L0_tok_b1
    w2 = zeros(FC + 2, 2, D)
    w2[0:FC, 0], w2[0:FC, 1] = L0_tok_W2[0:FC], L0_tok_W2[FC:D]
    w2[FC, 1], w2[FC + 1, 1] = L0_tok_b2, cls_tok[0, 0]
    lnp = np.stack([L0_tok_ln_w.reshape(2, FC).T, L0_tok_ln_b.reshape(2, FC).T], axis=2)
    wq1 = qkv_cols(np.concatenate([L0_attn_wq.T, L0_attn_wk.T, L0_attn_wv.T], axis=1))
    wqkv1 = wq1.reshape(2, FC, 3 * D).transpose(1, 0, 2)
    wq2 = qkv_cols(L0_ffn_Wqkv.T)
    wqkv2 = zeros(FC + 1 + EXPERTS, 2, 3 * D)
    wqkv2[0:FC] = wq2.reshape(2, FC, 3 * D).transpose(1, 0, 2)
    wqkv2[FC, 1] = qkv_cols(L0_ffn_bqkv[None])[0]
    wqkv2[FC + 1:, 1] = qkv_cols(L0_ffn_bb)
    wlora = qkv_cols(L0_ffn_Bm.transpose(0, 2, 1).reshape(ER, 3 * D))
    wgl = zeros(FC + 1, 2, ER + EXPERTS)
    wgl[0:FC, :, 0:ER] = L0_ffn_A.reshape(ER, D).T.reshape(2, FC, ER).transpose(1, 0, 2)
    wgl[0:FC, :, ER:] = L0_ffn_Wg.T.reshape(2, FC, EXPERTS).transpose(1, 0, 2)
    wgl[FC, 1, 0:ER], wgl[FC, 1, ER:] = L0_ffn_ba.reshape(ER), L0_ffn_bg

    def wo_rows(wt):
        r = zeros(GH, 32, GROUPS, D)
        r[:, 0:HD] = wt.reshape(GROUPS, GH, HD, D).transpose(1, 2, 0, 3)
        return r.reshape(128, GROUPS, D)

    wo1, wo2 = wo_rows(L0_attn_wo.T), wo_rows(L0_ffn_Wproj.T)
    wo2[HD, 0] = L0_ffn_bproj

    ident = np.eye(128, dtype=f)
    bf = mybir.dt.np(BF16) if hasattr(mybir.dt, "np") else __import__("ml_dtypes").bfloat16
    seq = [np.array(list(range(1, HALF + 1)) + [0]), np.arange(HALF)]
    masks = np.zeros((HALF + 1, 4, HALF + 1), f)
    for a in range(2):
        r = ROWS[a]
        late = np.where(seq[a][None, :] > seq[a][:, None], f(-1e9), f(0))
        masks[0:r, a, 0:r] = late
        masks[0:r, 2 + a, 0:r] = late.T
    sel = zeros(128, 128)
    for h in range(GH):
        sel[32 * h + HD, 32 * h:32 * h + 32] = 1
    marks = np.ones((2, PT), f)
    for b in range(2):
        marks[0, 2 * b * TR + HALF] = 0
    marks[1] = 1 - marks[0]
    rank8 = np.tile(np.arange(EXPERTS, 0, -1, dtype=f), (HALF + 1, 1))

    arrays = dict(x=x, w1=w1, w2=w2, lnp=lnp, wqkv1=wqkv1, wo1=wo1, wgl=wgl, wqkv2=wqkv2, wlora=wlora, wo2=wo2,
                  ident=ident, identb=ident.astype(bf), masks=masks.astype(bf), sel=sel, marks=marks, rank8=rank8)
    nc = bacc.Bacc("TRN2", target_bir_lowering=False, num_devices=1)
    named, args = {}, []
    for name, a in arrays.items():
        a = np.ascontiguousarray(a)
        named[f"in_{name}"] = a
        args.append(nc.dram_tensor(f"in_{name}", a.shape, mybir.dt.from_np(a.dtype), kind="ExternalInput").ap())
    out = nc.dram_tensor("out_0", (IMAGES, TOK, D), F32, kind="ExternalOutput").ap()
    vit_tower(nc, *args, out)
    r = run_bass_kernel_spmd(nc, [named], core_ids=[0])
    return r.results[0]["out_0"]
```
